# Optimizing a Trainium2 kernel written in Bass

```python
import numpy as np
import jax
import jax.numpy as jnp

def _softmax(x, axis=-1):
    return jax.nn.softmax(x, axis=axis)

def _gelu(x):
    return jax.nn.gelu(x, approximate=True)

def _silu(x):
    return jax.nn.silu(x)

def _sigmoid(x):
    return jax.nn.sigmoid(x)

def _layernorm(x, axis=-1, eps=1e-05):
    m = jnp.mean(x, axis=axis, keepdims=True)
    v = jnp.var(x, axis=axis, keepdims=True)
    return (x - m) / jnp.sqrt(v + eps)

def _scatter_add(tgt, idx, src, axis=0):
    return tgt.at[idx].add(src)

def _segment_sum(src, seg, n):
    return jax.ops.segment_sum(src, seg, n)
kernel_name = 'mk_decoder_preln_d1_seqx_r8_230709'

def setup_inputs(seed: int=0):
    np.random.seed(seed)
    _w = jnp.asarray

    def _rec_inputs():
        import jax
        import jax.numpy as jnp
        _rk = jax.random.key(seed)
        x = -0.0002928 + 1 * jax.random.normal(jax.random.fold_in(_rk, 1), (2, 256, 128), jnp.float32)
        _lenS = 256 - jax.random.randint(jax.random.fold_in(_rk, 7), (2,), 0, max(1, 256 // 4) + 1, jnp.int32)
        _lenS2 = 512 - jax.random.randint(jax.random.fold_in(_rk, 8), (2,), 0, max(1, 512 // 4) + 1, jnp.int32)
        _ctx_1024P = jax.random.normal(jax.random.fold_in(_rk, 11), (2, 16, 128), jnp.float32)
        _ctx_1024c = jax.random.dirichlet(jax.random.fold_in(_rk, 511), 0.3 * jnp.ones((16,), jnp.float32), (2, 512))
        _ctx_1024t = jnp.einsum('bsk,bkd->bsd', _ctx_1024c, _ctx_1024P)
        _ctx_1024t = _ctx_1024t * jax.lax.rsqrt(jnp.mean(jnp.square(_ctx_1024t)) + 1e-12) * 0.953939
        ctx_1024 = -1.39393e-06 + 0.999914 * (_ctx_1024t + 0.3 * jax.random.normal(jax.random.fold_in(_rk, 611), (2, 512, 128), jnp.float32))
        _validS = jnp.arange(256)[None, :] < _lenS[:, None]
        _validS2 = jnp.arange(512)[None, :] < _lenS2[:, None]
        _causal = jnp.tril(jnp.ones((256, 256), dtype=bool))
        mask_1x1xSxS2_ik1 = jnp.where(jnp.broadcast_to(_validS2[0:1, None, None, :], (1, 1, 256, 512)), 1, 0).astype(jnp.int32)
        return (x, ctx_1024, mask_1x1xSxS2_ik1)
    x, ctx_1024, mask_1x1xSxS2_ik1 = _rec_inputs()

    def _L0_attn_setup():
        import jax, jax.numpy as jnp
        import numpy as np
        NUM_HEADS = 16
        HIDDEN = 128
        ATTN_DIM = 64
        HEAD_OUT = 64
        OUT_DIM = 128
        BATCH, SEQ = (2, 256)

        def _split_heads(y, h):
            b, s, _ = y.shape
            return y.reshape(b, s, h, -1).transpose(0, 2, 1, 3)
        key = jax.random.key(seed)
        ks = jax.random.split(key, 9)
        s_in = 1.0 / np.sqrt(HIDDEN)
        s_o = 1.0 / np.sqrt(NUM_HEADS * HEAD_OUT)
        return {'x': jax.random.normal(ks[0], (BATCH, SEQ, HIDDEN), dtype=jnp.float32), 'Wq': jax.random.uniform(ks[1], (HIDDEN, NUM_HEADS * ATTN_DIM), jnp.float32, -s_in, s_in), 'bq': jax.random.uniform(ks[2], (NUM_HEADS * ATTN_DIM,), jnp.float32, -s_in, s_in), 'Wk': jax.random.uniform(ks[3], (HIDDEN, NUM_HEADS * ATTN_DIM), jnp.float32, -s_in, s_in), 'bk': jax.random.uniform(ks[4], (NUM_HEADS * ATTN_DIM,), jnp.float32, -s_in, s_in), 'Wv': jax.random.uniform(ks[5], (HIDDEN, NUM_HEADS * HEAD_OUT), jnp.float32, -s_in, s_in), 'bv': jax.random.uniform(ks[6], (HIDDEN, NUM_HEADS * HEAD_OUT)[1:], jnp.float32, -s_in, s_in), 'Wo': jax.random.uniform(ks[7], (NUM_HEADS * HEAD_OUT, OUT_DIM), jnp.float32, -s_o, s_o), 'bo': jax.random.uniform(ks[8], (OUT_DIM,), jnp.float32, -s_o, s_o)}
    _L0_attn_all = _L0_attn_setup()
    _L0_attn_in = {k: v for k, v in _L0_attn_all.items() if k in ('Wq', 'bq', 'Wk', 'bk', 'Wv', 'bv', 'Wo', 'bo')}
    del _L0_attn_all

    def _L0_xattn_setup():
        import jax, jax.numpy as jnp
        import numpy as np
        B, S, D, H = (2, 256, 128, 16)
        HD = D // H
        key = jax.random.key(seed)
        ks = jax.random.split(key, 8)
        s = 0.02
        return {'Q': jax.random.normal(ks[0], (B, S, D), jnp.float32), 'K': jax.random.normal(ks[1], (B, S, D), jnp.float32), 'V': jax.random.normal(ks[2], (B, S, D), jnp.float32), 'mask': jax.random.randint(ks[3], (1, 1, S, S), 0, 2, jnp.int32), 'Wq': jax.random.normal(ks[4], (D, D), jnp.float32) * s, 'bq': jnp.zeros((D,), jnp.float32), 'Wk': jax.random.normal(ks[5], (D, D), jnp.float32) * s, 'bk': jnp.zeros((D,), jnp.float32), 'Wv': jax.random.normal(ks[6], (D, D), jnp.float32) * s, 'bv': jnp.zeros((D,), jnp.float32), 'Wo': jax.random.normal(ks[7], (D, D), jnp.float32) * s, 'bo': jnp.zeros((D,), jnp.float32)}
    _L0_xattn_all = _L0_xattn_setup()
    _L0_xattn_in = {k: v for k, v in _L0_xattn_all.items() if k in ('Wq', 'bq', 'Wk', 'bk', 'Wv', 'bv', 'Wo', 'bo')}
    del _L0_xattn_all

    def _L0_ffn_setup():
        import jax, jax.numpy as jnp
        import numpy as np
        B, S, H = (4, 256, 128)
        D = 256
        E = 8
        K = 2
        key = jax.random.key(seed)
        ks = jax.random.split(key, 8)
        w = lambda k, shape: jax.random.normal(k, shape, jnp.float32) * 0.02
        return {'hidden_states': jax.random.normal(ks[0], (B, S, H), jnp.float32), 'gate_w': w(ks[1], (H, E)), 'w_gate': w(ks[2], (E, H, D)), 'w_up': w(ks[3], (E, H, D)), 'w_down': w(ks[4], (E, D, H)), 'ws_gate': w(ks[5], (H, D)), 'ws_up': w(ks[6], (H, D)), 'ws_down': w(ks[7], (D, H))}
    _L0_ffn_all = _L0_ffn_setup()
    _L0_ffn_in = {k: v for k, v in _L0_ffn_all.items() if k in ('gate_w', 'w_gate', 'w_up', 'w_down', 'ws_gate', 'ws_up', 'ws_down')}
    del _L0_ffn_all
    return {'x': x, 'ctx_1024': ctx_1024, 'mask_1x1xSxS2_ik1': mask_1x1xSxS2_ik1, 'L0_attn_Wq': _L0_attn_in['Wq'], 'L0_attn_bq': _L0_attn_in['bq'], 'L0_attn_Wk': _L0_attn_in['Wk'], 'L0_attn_bk': _L0_attn_in['bk'], 'L0_attn_Wv': _L0_attn_in['Wv'], 'L0_attn_bv': _L0_attn_in['bv'], 'L0_attn_Wo': _L0_attn_in['Wo'], 'L0_attn_bo': _L0_attn_in['bo'], 'L0_xattn_Wq': _L0_xattn_in['Wq'], 'L0_xattn_bq': _L0_xattn_in['bq'], 'L0_xattn_Wk': _L0_xattn_in['Wk'], 'L0_xattn_bk': _L0_xattn_in['bk'], 'L0_xattn_Wv': _L0_xattn_in['Wv'], 'L0_xattn_bv': _L0_xattn_in['bv'], 'L0_xattn_Wo': _L0_xattn_in['Wo'], 'L0_xattn_bo': _L0_xattn_in['bo'], 'L0_ffn_gate_w': _L0_ffn_in['gate_w'], 'L0_ffn_w_gate': _L0_ffn_in['w_gate'], 'L0_ffn_w_up': _L0_ffn_in['w_up'], 'L0_ffn_w_down': _L0_ffn_in['w_down'], 'L0_ffn_ws_gate': _L0_ffn_in['ws_gate'], 'L0_ffn_ws_up': _L0_ffn_in['ws_up'], 'L0_ffn_ws_down': _L0_ffn_in['ws_down']}

def reference(x, ctx_1024, mask_1x1xSxS2_ik1, L0_attn_Wq, L0_attn_bq, L0_attn_Wk, L0_attn_bk, L0_attn_Wv, L0_attn_bv, L0_attn_Wo, L0_attn_bo, L0_xattn_Wq, L0_xattn_bq, L0_xattn_Wk, L0_xattn_bk, L0_xattn_Wv, L0_xattn_bv, L0_xattn_Wo, L0_xattn_bo, L0_ffn_gate_w, L0_ffn_w_gate, L0_ffn_w_up, L0_ffn_w_down, L0_ffn_ws_gate, L0_ffn_ws_up, L0_ffn_ws_down):
    import jax
    import jax.numpy as jnp

    def _L0_attn_ref(x, Wq, bq, Wk, bk, Wv, bv, Wo, bo):
        import jax, jax.numpy as jnp
        import numpy as np
        NUM_HEADS = 16
        HIDDEN = 128
        ATTN_DIM = 64
        HEAD_OUT = 64
        OUT_DIM = 128
        BATCH, SEQ = (2, 256)

        def _split_heads(y, h):
            b, s, _ = y.shape
            return y.reshape(b, s, h, -1).transpose(0, 2, 1, 3)
        h = NUM_HEADS
        q = _split_heads(x @ Wq + bq, h)
        k = _split_heads(x @ Wk + bk, h)
        v = _split_heads(x @ Wv + bv, h)
        scale = 1.0 / jnp.sqrt(jnp.float32(ATTN_DIM))
        pattern = jnp.einsum('bhid,bhjd->bhij', k, q) * scale
        prob = jax.nn.softmax(pattern, axis=-2)
        out = jnp.einsum('bhis,bhid->bhsd', prob, v)
        b, _, s, dv = out.shape
        concat = out.transpose(0, 2, 1, 3).reshape(b, s, h * dv)
        return concat @ Wo + bo

    def _L0_xattn_ref(Q, K, V, mask, Wq, bq, Wk, bk, Wv, bv, Wo, bo):
        import jax, jax.numpy as jnp
        import numpy as np
        B, S, D, H = (2, 256, 128, 16)
        HD = D // H
        b = Q.shape[0]
        q = (Q @ Wq + bq).reshape(b, -1, H, HD).transpose(0, 2, 1, 3)
        k = (K @ Wk + bk).reshape(b, -1, H, HD).transpose(0, 2, 1, 3)
        v = (V @ Wv + bv).reshape(b, -1, H, HD).transpose(0, 2, 1, 3)
        scale = jnp.sqrt(jnp.asarray(HD, q.dtype))
        scores = jnp.einsum('bhqd,bhkd->bhqk', q, k) / scale
        scores = jnp.where(mask == 0, -jnp.inf, scores)
        attn = jax.nn.softmax(scores, axis=-1)
        ctx = jnp.einsum('bhqk,bhkd->bhqd', attn, v)
        concat = ctx.transpose(0, 2, 1, 3).reshape(b, -1, H * HD)
        return concat @ Wo + bo

    def _L0_ffn_ref(hidden_states, gate_w, w_gate, w_up, w_down, ws_gate, ws_up, ws_down):
        import jax, jax.numpy as jnp
        import numpy as np
        B, S, H = (4, 256, 128)
        D = 256
        E = 8
        K = 2
        b, s, h = hidden_states.shape
        x = hidden_states.reshape(-1, h)
        scores = jax.nn.softmax(x @ gate_w, axis=-1)
        topk_w, topk_idx = jax.lax.top_k(scores, K)
        topk_w = topk_w / (jnp.sum(topk_w, axis=-1, keepdims=True) + 1e-20)
        onehot = jax.nn.one_hot(topk_idx, E, dtype=x.dtype)
        w_per_expert = jnp.einsum('nke,nk->ne', onehot, topk_w)
        y = jnp.zeros_like(x)
        for e in range(E):
            hid = jax.nn.silu(x @ w_gate[e]) * (x @ w_up[e])
            y = y + w_per_expert[:, e:e + 1] * (hid @ w_down[e])
        shared = jax.nn.silu(x @ ws_gate) * (x @ ws_up) @ ws_down
        return (y + shared).reshape(b, s, h)
    x = x + _L0_attn_ref(_layernorm(x, axis=-1), L0_attn_Wq, L0_attn_bq, L0_attn_Wk, L0_attn_bk, L0_attn_Wv, L0_attn_bv, L0_attn_Wo, L0_attn_bo)
    x = x + _L0_xattn_ref(_layernorm(x, axis=-1), ctx_1024, ctx_1024, mask_1x1xSxS2_ik1, L0_xattn_Wq, L0_xattn_bq, L0_xattn_Wk, L0_xattn_bk, L0_xattn_Wv, L0_xattn_bv, L0_xattn_Wo, L0_xattn_bo)
    x = x + _L0_ffn_ref(_layernorm(x, axis=-1), L0_ffn_gate_w, L0_ffn_w_gate, L0_ffn_w_up, L0_ffn_w_down, L0_ffn_ws_gate, L0_ffn_ws_up, L0_ffn_ws_down)
    return x

_drawn_inputs = setup_inputs


def setup_inputs(seed=0):
    import zlib

    import numpy as np

    out = dict(_drawn_inputs(seed))
    spreads = {'L0_xattn_bq': (0.0, 0.8),
     'L0_xattn_bk': (0.0, 0.8),
     'L0_xattn_bv': (0.0, 0.388),
     'L0_xattn_bo': (0.0, 0.1)}
    factors = {'L0_attn_Wq': 4.736,
     'L0_attn_bq': 8.0,
     'L0_attn_Wk': 4.729,
     'L0_attn_bk': 8.0,
     'L0_attn_bo': 3.016,
     'L0_xattn_Wq': 8.0,
     'L0_xattn_Wk': 8.0,
     'L0_ffn_gate_w': 8.0,
     'L0_ffn_w_gate': 8.0,
     'L0_ffn_w_up': 8.0,
     'L0_ffn_w_down': 8.0,
     'L0_ffn_ws_gate': 6.956,
     'L0_ffn_ws_up': 6.879,
     'L0_ffn_ws_down': 6.906}
    for name, (base, spread) in spreads.items():
        noise = np.random.default_rng([zlib.crc32(name.encode()), seed]).standard_normal(out[name].shape)
        drawn = base * np.exp(spread * noise) if base else spread * noise
        out[name] = jnp.asarray(drawn.astype(out[name].dtype))
    for name, factor in factors.items():
        out[name] = (out[name] * factor).astype(out[name].dtype)
    return out
```

```python
from contextlib import ExitStack

import concourse.bass as bass
from concourse import mybir

F32 = mybir.dt.float32
BF16 = mybir.dt.bfloat16
ALU = mybir.AluOpType
ACT = mybir.ActivationFunctionType
AX = mybir.AxisListType

P = 128
B, S, D = 2, 256, 128
C = S // P
NC_ = B * C
T = B * S
H1, HD1 = 16, 64
NP = H1 // 2
H2, HD2 = 16, 8
SK = 512
KC = SK // P
TK = B * SK
PARTS = 3
KSTACK = PARTS * PARTS * HD2
HG = 4
NG = H2 // HG
CW = P // HG
NE, FF = 8, 256
FC = FF // P
EPS = 1e-5
MASKED = 1e30
BANK = 512
SCALE1 = 1.0 / 8.0
SCALE2 = float(HD2) ** -0.5
PT_SLOTS = 6

PT_BANK, O_BANK, MID_BANK = 4, 6, 7

SELF_MID = {10: ("wo", 0), 12: ("turn", 0), 13: ("q", 0)}
CROSS_MID = {1: ("wo", 1), 3: ("turn", 1), 5: ("q", 1), 20: ("wo2", 0), 23: ("turn2", 0)}
N_SELF = B * NP
N_CROSS = B * H2


def items():
    out = [("ctx_t", 0, "act"), ("ctx_t", 1, "act"), ("kx", 0, "act"), ("kx", 1, "act"),
           ("vx", 0, "act"), ("vx", 1, "act"), ("x_t", 0, "act")]
    for p in range(NP):
        out += [("q", p, "act"), ("k", p, "dve")]
    for c in range(NC_):
        out += [("v", (c, 0), "act"), ("v", (c, 1), "dve")]
    return out


ITEMS = items()


def evacuated(j):
    engine = ITEMS[j][2]
    return engine, sum(1 for x in ITEMS[:j + 1] if x[2] == engine)


def index_of(kind, which):
    return [x[:2] for x in ITEMS].index((kind, which))


def build(nc, a, out):
    with ExitStack() as ctx:
        def sb(name, shape, dt=F32):
            return ctx.enter_context(nc.sbuf_tensor(name, shape, dt))

        def sem(name):
            return ctx.enter_context(nc.semaphore(name))

        ps = ctx.enter_context(nc.psum_tensor("ps", [P, 8, BANK], F32))

        ident = sb("ident", [P, P])
        x_in = sb("x_in", [P, NC_, D])
        x_bo = sb("x_bo", [P, NC_, D])
        x1 = sb("x1", [P, NC_, D])
        x1_bo = sb("x1_bo", [P, NC_, D])
        x2 = sb("x2", [P, NC_, D])
        bo1 = sb("bo1", [P, D])
        bo2 = sb("bo2", [P, D])
        stats = sb("stats", [P, NC_, 6])
        mean_var = sb("mean_var", [P, NC_, 2])
        var_eps = sb("var_eps", [P, NC_])
        minus_half = sb("minus_half", [P, NC_])
        rstd = sb("rstd", [P, NC_])
        x_hat = sb("x_hat", [P, NC_, D])
        x_hat_t = sb("x_hat_t", [P, T])
        w_in1 = sb("w_in1", [P, 3, H1 * HD1])
        wq1, wk1, wv1 = (w_in1[:, i, :] for i in range(3))
        wo1 = sb("wo1", [P, NP, D])
        bias1 = sb("bias1", [P, 3, NP])
        bq1_s = sb("bq1_s", [P, NP])
        q1_t = sb("q1_t", [P, NP, T])
        k1_t = sb("k1_t", [P, NP, T])
        v1 = sb("v1", [P, NC_, H1 * HD1])
        o1_t = sb("o1_t", [P, NP, T])
        low1 = sb("low1", [P, 2, 2, C])
        sum1 = sb("sum1", [P, 2, 2, C])
        rec1 = sb("rec1", [P, 2, 2, C])
        prob1 = sb("prob1", [P, 2, 2, C * S])
        prob1_t = sb("prob1_t", [P, 2, 2, C * S])
        prob1_flat = prob1[:, :, :, :].rearrange("p a r n -> p (a r n)")
        prob1_t_flat = prob1_t[:, :, :, :].rearrange("p a r n -> p (a r n)")

        k2_parts = prob1_flat[:, 0:PARTS * TK // 2].bitcast(BF16).rearrange("p (j t) -> p j t", j=PARTS)
        mask_in = prob1_t_flat[:, 0:C * SK].bitcast(mybir.dt.int32).rearrange("p (c k) -> p c k", c=C)
        ctx_in = prob1_t_flat[:, C * SK:C * SK + B * KC * D].rearrange("p (c d) -> p c d", d=D)
        context = sb("context", [P, 3, TK])
        ctx_t, k2_t, k2_rest = (context[:, i, :] for i in range(3))
        wq2 = sb("wq2", [P, D])
        wk2 = sb("wk2", [P, D])
        wv2 = sb("wv2", [P, D])
        wo2 = sb("wo2", [P, NG, D])
        bias2 = sb("bias2", [P, 2])
        bv2 = sb("bv2", [P, NG])
        mask_add = sb("mask_add", [P, C, SK])
        q2_t = sb("q2_t", [P, S])
        q2_rest = sb("q2_rest", [P, S])
        q2_parts = sb("q2_parts", [P, PARTS, S], BF16)
        k2_stack = sb("k2_stack", [KSTACK, H2, TK], BF16)
        q2_stack = sb("q2_stack", [KSTACK, H2, T], BF16)
        v2 = sb("v2", [P, B * KC, H2, CW])
        low2 = sb("low2", [P, 2, C])
        sum2 = sb("sum2", [P, 2, C, HG])
        rec2 = sb("rec2", [P, 2, C, HG])
        rec2_wide = sb("rec2_wide", [P, 2, C, P])
        rec2_t = sb("rec2_t", [P, S])
        score2 = prob1_flat.rearrange("p (a c k) -> p a c k", a=2, c=C)
        prob2 = prob1_t_flat.rearrange("p (a c k) -> p a c k", a=2, c=C)
        prob2_t = [q1_t[:, 2 * i:2 * i + 2, :] for i in range(4)] + [k1_t[:, 2 * i:2 * i + 2, :] for i in range(2)]
        prob2_t = [x.rearrange("p a (k t) -> p (a k) t", t=S) for x in prob2_t]
        o2_t = k1_t[:, 4:8, :]

        gate_w = sb("gate_w", [P, NE])
        wg, wu = (t[:, :, :].rearrange("p a n -> p (a n)")[:, 0:(NE + 1) * FF].rearrange("p (e f) -> p e f", f=FF)
                  for t in (w_in1, context))
        wd = v1[:, :, :].rearrange("p c n -> p (c n)")[:, 0:(NE + 1) * FC * D]\
            .rearrange("p (e f n) -> p e f n", e=NE + 1, f=FC)
        silu = q1_t[:, 0:4, :].rearrange("p (a f) t -> p a (f t)", a=2)
        hid = q1_t[:, 4:8, :].rearrange("p (a f) t -> p a f t", a=2)
        y_part = k1_t[:, 0:2, :].rearrange("p a (c n) -> p a c n", c=NC_)
        acc = k1_t[:, 2, :].rearrange("p (c n) -> p c n", c=NC_)
        y_out = k1_t[:, 3, :].rearrange("p (c n) -> p c n", c=NC_)
        rank = sb("rank", [P, NC_, NE])
        logit = sb("logit", [P, NC_, NE])
        gate_e = sb("gate_e", [P, NC_, NE])
        gate_s = sb("gate_s", [P, NC_, NE])
        pick = sb("pick", [P, NC_, NE])
        pick1 = sb("pick1", [P, NC_, NE])
        pick2 = sb("pick2", [P, NC_, NE])
        rest = sb("rest", [P, NC_, NE])
        w_e = sb("w_e", [P, NC_, NE])
        col = sb("col", [P, 6, NC_])

        k2_dram = nc.dram_tensor("k2_dram", [PARTS, D, TK], BF16, kind="Internal").ap()
        q2_dram = nc.dram_tensor("q2_dram", [B, PARTS, D, S], BF16, kind="Internal").ap()

        d_x, d_ctx, d_wk2, d_wv2, d_wq2 = map(sem, ("d_x", "d_ctx", "d_wk2", "d_wv2", "d_wq2"))
        d_wq1, d_wk1, d_wv1, d_wo1 = map(sem, ("d_wq1", "d_wk1", "d_wv1", "d_wo1"))
        d_bias, d_mask, d_bo, d_pad, d_ffn, d_wd = map(sem, ("d_bias", "d_mask", "d_bo", "d_pad", "d_ffn", "d_wd"))
        d_kdram, d_kstack, d_out = map(sem, ("d_kdram", "d_kstack", "d_out"))
        d_qdram = [sem(f"d_qdram{b}") for b in range(B)]
        d_qstack = [sem(f"d_qstack{b}") for b in range(B)]
        s_pad0, s_const, s_ident = map(sem, ("s_pad0", "s_const", "s_ident"))
        s_dve, s_pool = map(sem, ("s_dve", "s_pool"))
        s_item = sem("s_item")
        s_ev = {"act": sem("s_ev_act"), "dve": sem("s_ev_dve")}
        s_bq = sem("s_bq")
        s_var, s_rstd, s_xhat, s_xhat_ps, s_xhat_t = map(sem, ("s_var", "s_rstd", "s_xhat", "s_xhat_ps", "s_xhat_t"))
        s_kparts, s_qparts, s_maskadd = map(sem, ("s_kparts", "s_qparts", "s_maskadd"))
        s_xbo, s_x1, s_x1bo, s_x2 = map(sem, ("s_xbo", "s_x1", "s_x1bo", "s_x2"))
        s_score1, s_low1, s_exp1, s_rec1, s_norm1 = map(sem, ("s_score1", "s_low1", "s_exp1", "s_rec1", "s_norm1"))
        s_turn1, s_pt1, s_pv1, s_o1 = map(sem, ("s_turn1", "s_pt1", "s_pv1", "s_o1"))
        s_wo, s_q2ps = map(sem, ("s_wo", "s_q2ps"))
        s_wide2 = sem("s_wide2")
        s_score2, s_low2, s_exp2, s_rec2 = map(sem, ("s_score2", "s_low2", "s_exp2", "s_rec2"))
        s_turn2a, s_turn2b, s_pt2a, s_pt2b = map(sem, ("s_turn2a", "s_turn2b", "s_pt2a", "s_pt2b"))
        s_pv2, s_rec2ps, s_rec2t, s_o2n, s_o2 = map(sem, ("s_pv2", "s_rec2ps", "s_rec2t", "s_o2n", "s_o2"))
        s_logit, s_lshift, s_gexp, s_we = map(sem, ("s_logit", "s_lshift", "s_gexp", "s_we"))
        s_g, s_u, s_silu, s_hid, s_y, s_ypart, s_acc, s_out = map(sem, (
            "s_g", "s_u", "s_silu", "s_hid", "s_y", "s_ypart", "s_acc", "s_out"))

        def chunks(ap):
            return ap.rearrange("b (c p) d -> p (b c) d", p=P)

        block = ctx.enter_context(nc.Block())

        @block.sync
        def _(sp):
            def load(dst, src, s):
                sp.dma_start(dst, src).then_inc(s, 16)

            load(ctx_in, chunks(a["ctx_1024"]), d_ctx)
            load(x_in[:, :, :], chunks(a["x"]), d_x)
            load(wk2[:, :], a["L0_xattn_Wk"], d_wk2)
            load(wv2[:, :], a["L0_xattn_Wv"], d_wv2)
            load(wq1, a["L0_attn_Wq"], d_wq1)
            load(wk1, a["L0_attn_Wk"], d_wk1)
            load(wv1, a["L0_attn_Wv"], d_wv1)
            load(mask_in, a["mask_1x1xSxS2_ik1"].rearrange("a b (c p) k -> p (a b c) k", p=P), d_mask)
            load(wq2[:, :], a["L0_xattn_Wq"], d_wq2)
            load(wo1[:, :, :], a["L0_attn_Wo"].rearrange("(p r) n -> r p n", r=P), d_wo1)
            sp.wait_ge(s_kparts, 1)
            load(k2_dram.rearrange("j r t -> r j t"), k2_parts, d_kdram)
            sp.wait_ge(d_kdram, 16)
            for i in range(PARTS):
                for j in range(PARTS):
                    r = (i * PARTS + j) * HD2
                    load(k2_stack[r:r + HD2, :, :], k2_dram[j].rearrange("(h d) t -> d h t", d=HD2), d_kstack)
            sp.wait_ge(s_item, len(ITEMS))
            load(wg[:, 0:NE, :], a["L0_ffn_w_gate"].rearrange("e d f -> d e f"), d_ffn)
            load(wu[:, 0:NE, :], a["L0_ffn_w_up"].rearrange("e d f -> d e f"), d_ffn)
            load(wg[:, NE, :], a["L0_ffn_ws_gate"], d_ffn)
            load(wu[:, NE, :], a["L0_ffn_ws_up"], d_ffn)
            load(gate_w[:, :], a["L0_ffn_gate_w"], d_ffn)
            for b in range(B):
                sp.wait_ge(s_qparts, b + 1)
                load(q2_dram[b].rearrange("i r t -> r i t"), q2_parts[:, :, :], d_qdram[b])
                sp.wait_ge(d_qdram[b], 16)
                for i in range(PARTS):
                    for j in range(PARTS):
                        r = (i * PARTS + j) * HD2
                        load(q2_stack[r:r + HD2, :, b * S:(b + 1) * S],
                             q2_dram[b, i].rearrange("(h d) t -> d h t", d=HD2), d_qstack[b])
                if b == 0:
                    sp.wait_ge(s_pv1, N_SELF)
                    load(wd[:, 0:NE, :, :], a["L0_ffn_w_down"].rearrange("e (f r) n -> r e f n", r=P), d_wd)
                    load(wd[:, NE, :, :], a["L0_ffn_ws_down"].rearrange("(f r) n -> r f n", r=P), d_wd)
            out_c = chunks(out)
            for c in range(NC_):
                sp.wait_ge(s_out, c + 1)
                load(out_c[:, c, :], y_out[:, c, :], d_out)
            sp.wait_ge(d_out, 16 * NC_)

        @block.gpsimd
        def _(pool):
            chain = [0]

            def link(ins):
                chain[0] += 1
                ins.then_inc(s_pool, 1)
                pool.wait_ge(s_pool, chain[0])

            link(nc.gpsimd.memset(ident[:, :], 0.0))
            nc.gpsimd.affine_select(out=ident[:, :], in_=ident[:, :], compare_op=ALU.not_equal, fill=1.0,
                                    base=0, pattern=[[-1, P]], channel_multiplier=1).then_inc(s_ident, 1)
            for name, i in (("L0_attn_bq", 0), ("L0_attn_bk", 1), ("L0_attn_bv", 2)):
                pool.dma_start(bias1[:, i, :], a[name]).then_inc(d_bias, 16)
            for name, i in (("L0_xattn_bq", 0), ("L0_xattn_bk", 1)):
                pool.dma_start(bias2[:, i:i + 1], a[name].rearrange("(r o) -> r o", o=1)).then_inc(d_bias, 16)
            link(nc.gpsimd.memset(minus_half[:, :], -0.5))

            def reciprocal_std(k, first, count):
                pool.wait_ge(s_var, k + 1)
                link(nc.gpsimd.tensor_scalar(var_eps[:, first:first + count], mean_var[:, first:first + count, 1],
                                             EPS, None, ALU.add))
                nc.gpsimd.tensor_tensor(rstd[:, first:first + count], var_eps[:, first:first + count],
                                        minus_half[:, first:first + count], ALU.pow).then_inc(s_rstd, 1)

            reciprocal_std(0, 0, NC_)
            nc.gpsimd.memset(wo2[:, :, :], 0.0).then_inc(s_pad0, 1)
            nc.gpsimd.memset(bv2[:, :], 0.0).then_inc(s_pad0, 1)
            nc.gpsimd.memset(v2[:, :, :, :], 0.0).then_inc(s_const, 1)
            for e in range(NE):
                nc.gpsimd.memset(rank[:, :, e], float(NE - e)).then_inc(s_const, 1)
            pool.dma_start(bo1[:, :], a["L0_attn_bo"].rearrange("(o n) -> o n", o=1).to_broadcast([P, D])).then_inc(d_bo, 16)
            pool.dma_start(bo2[:, :], a["L0_xattn_bo"].rearrange("(o n) -> o n", o=1).to_broadcast([P, D])).then_inc(d_bo, 16)
            pool.wait_ge(s_pad0, 2)
            for g in range(HG):
                rows = slice(CW * g, CW * g + HD2)
                pool.dma_start(wo2[rows, :, :], a["L0_xattn_Wo"].rearrange("(k g d) n -> g d k n", g=HG, d=HD2)[g]
                               ).then_inc(d_pad, 16)
                pool.dma_start(bv2[rows, :], a["L0_xattn_bv"][g]
                               ).then_inc(d_pad, 16)
            pool.wait_ge(d_x, 16)
            pool.wait_ge(d_bo, 32)
            for c in range(NC_):
                nc.gpsimd.tensor_tensor(x_bo[:, c, :], x_in[:, c, :], bo1[:, :], ALU.add).then_inc(s_xbo, 1)

            def add_bo2(b):
                pool.wait_ge(s_x1, b + 1)
                for c in range(b * C, (b + 1) * C):
                    nc.gpsimd.tensor_tensor(x1_bo[:, c, :], x1[:, c, :], bo2[:, :], ALU.add).then_inc(s_x1bo, 1)

            for s in range(N_SELF):
                for r in range(2):
                    pool.wait_ge(s_rec1, 2 * s + r + 1)
                    pr = prob1[:, s % 2, r, :].rearrange("p (c i) -> p c i", c=C)
                    nc.gpsimd.tensor_tensor(pr, pr, rec1[:, s % 2, r, :].unsqueeze(2).to_broadcast([P, C, S]),
                                            ALU.mult).then_inc(s_norm1, 1)
                if SELF_MID.get(s + 1) == ("wo", 0):
                    reciprocal_std(1, 0, C)
                    add_bo2(0)

            def add_bv2(b, hg):
                k = b * NG + hg
                pool.wait_ge(s_o2n, k + 1)
                o = o2_t[:, hg, b * S:(b + 1) * S]
                nc.gpsimd.tensor_scalar(o, o, bv2[:, hg:hg + 1], None, ALU.add).then_inc(s_o2, 1)

            def widen(k):
                pool.wait_ge(s_rec2, k + 1)
                if k >= 2:
                    pool.wait_ge(s_rec2ps, k - 1)
                nc.gpsimd.tensor_copy(rec2_wide[:, k % 2, :, :].rearrange("p c (g d) -> p c g d", g=HG),
                                      rec2[:, k % 2, :, :].unsqueeze(3).to_broadcast([P, C, HG, CW])
                                      ).then_inc(s_wide2, 1)

            reciprocal_std(2, C, C)
            add_bo2(1)
            pool.wait_ge(d_pad, 32 * HG)
            for k in range(B * NG):
                widen(k)
                if k == NG:
                    reciprocal_std(3, 0, C)
                add_bv2(*divmod(k, NG))
            reciprocal_std(4, C, C)
            for k in range(1, NE):
                pool.wait_ge(s_ypart, k + 1)
                if k > 1:
                    pool.wait_ge(s_acc, k - 1)
                nc.gpsimd.tensor_tensor(acc, acc, y_part[:, k % 2], ALU.add).then_inc(s_acc, 1)

        @block.scalar
        def _(act):
            act.wait_ge(d_bias, 16 * 5)
            nc.scalar.mul(bq1_s[:, :], bias1[:, 0, :], -SCALE1).then_inc(s_bq, 1)

            def evacuate(j, kind, which):
                act.wait_ge(s_item, j + 1)
                bank = ps[:, j % 8, :]
                if kind == "ctx_t":
                    ins = nc.scalar.copy(ctx_t[:, which * BANK:(which + 1) * BANK], bank)
                elif kind == "kx":
                    ins = nc.scalar.activation(k2_t[:, which * BANK:(which + 1) * BANK], bank, ACT.Identity,
                                               bias=bias2[:, 1:2])
                elif kind == "vx":
                    if which == 0:
                        act.wait_ge(s_const, 1 + NE)
                    ins = nc.scalar.copy(v2[:, which * KC:(which + 1) * KC, :, 0:HD2],
                                         bank.rearrange("p (c h d) -> p c h d", c=KC, h=H2))
                elif kind == "x_t":
                    ins = nc.scalar.copy(x_hat_t[:, :], bank)
                elif kind == "q":
                    if which == 0:
                        act.wait_ge(s_bq, 1)
                    ins = nc.scalar.activation(q1_t[:, which, :], bank, ACT.Identity,
                                               bias=bq1_s[:, which:which + 1], scale=-SCALE1)
                else:
                    c, half = which
                    ins = nc.scalar.copy(v1[:, c, half * BANK:(half + 1) * BANK], bank)
                ins.then_inc(s_ev["act"], 1)

            for j, (kind, which, engine) in enumerate(ITEMS):
                if engine == "act":
                    evacuate(j, kind, which)

            def x_hat_evac(k, b):
                act.wait_ge(s_xhat_ps, k)
                nc.scalar.copy(x_hat_t[:, b * S:(b + 1) * S], ps[:, MID_BANK, 0:S]).then_inc(s_xhat_t, 1)

            act.wait_ge(d_kdram, 16)
            for s in range(N_SELF + 2):
                if s < N_SELF:
                    for r in range(2):
                        act.wait_ge(s_low1, 2 * s + r + 1)
                        if s >= 2:
                            act.wait_ge(s_turn1, 2 * (s - 2) + r + 1)
                        for c in range(C):
                            e = nc.scalar.activation(prob1[:, s % 2, r, c * S:(c + 1) * S],
                                                     ps[:, 2 * (s % 2) + r, c * S:(c + 1) * S], ACT.Exp,
                                                     bias=low1[:, s % 2, r, c:c + 1], scale=-1.0,
                                                     accum_out=sum1[:, s % 2, r, c:c + 1])
                        e.then_inc(s_exp1, 1)
                if s >= 2:
                    b, p = divmod(s - 2, NP)
                    act.wait_ge(s_pv1, s - 1)
                    nc.scalar.activation(o1_t[:, p, b * S:(b + 1) * S], ps[:, O_BANK, 0:S], ACT.Identity,
                                         bias=bias1[:, 2, p:p + 1]).then_inc(s_o1, 1)
                if SELF_MID.get(s) == ("turn", 0):
                    x_hat_evac(1, 0)

            for n in range(N_CROSS + 3):
                if n < N_CROSS:
                    for c in range(C):
                        act.wait_ge(s_low2, C * n + c + 1)
                        if n >= 2 and c == 0:
                            act.wait_ge(s_turn2b, n - 1)
                        if n % HG == 0 and c == 0 and n >= 2 * HG:
                            act.wait_ge(s_rec2, n // HG - 1)
                        nc.scalar.activation(prob2[:, n % 2, c, :], score2[:, n % 2, c, :], ACT.Exp,
                                             bias=low2[:, n % 2, c:c + 1], scale=-1.0,
                                             accum_out=sum2[:, n // HG % 2, c, n % HG:n % HG + 1]
                                             ).then_inc(s_exp2, 1)
                if 1 <= n <= N_CROSS:
                    act.wait_ge(s_turn2b, n)
                    nc.scalar.copy(prob2_t[(n - 1) % PT_SLOTS][:, 2:4, :],
                                   ps[:, PT_BANK + 1, :].rearrange("p (k t) -> p k t", k=2)).then_inc(s_pt2b, 1)
                if n % HG == 1 and n > HG:
                    k = (n - HG - 1) // HG
                    act.wait_ge(s_rec2ps, k + 1)
                    nc.scalar.copy(rec2_t[:, :], ps[:, O_BANK, S:2 * S]).then_inc(s_rec2t, 1)
                mid = CROSS_MID.get(n)
                if mid == ("turn", 1):
                    x_hat_evac(2, 1)
                if mid == ("turn2", 0):
                    x_hat_evac(3, 0)
            x_hat_evac(4, 1)

            act.wait_ge(s_lshift, 1)
            nc.scalar.activation(gate_e[:, :, :], logit[:, :, :], ACT.Exp).then_inc(s_gexp, 1)
            for k in range(NE + 1):
                act.wait_ge(s_g, k + 1)
                if k >= 2:
                    act.wait_ge(s_hid, k - 1)
                nc.scalar.activation(silu[:, k % 2, :], ps[:, 0:2, :].rearrange("p f t -> p (f t)"), ACT.Silu
                                     ).then_inc(s_silu, 1)

        @block.tensor
        def _(pe):
            mm, turn = nc.tensor.matmul, nc.tensor.transpose
            pe.wait_ge(s_ident, 1)
            for j, (kind, which, _) in enumerate(ITEMS):
                bank = ps[:, j % 8, :]
                if j >= 8:
                    engine, value = evacuated(j - 8)
                    pe.wait_ge(s_ev[engine], value)
                if kind == "ctx_t":
                    if which == 0:
                        pe.wait_ge(d_ctx, 16)
                    for c in range(KC):
                        last = turn(bank[:, c * P:(c + 1) * P], ctx_in[:, which * KC + c, :], ident[:, :])
                elif kind == "kx":
                    if which == 0:
                        pe.wait_ge(d_wk2, 16)
                        pe.wait_ge(s_ev["act"], 2)
                    last = mm(bank, wk2[:, :], ctx_t[:, which * BANK:(which + 1) * BANK], start=True, stop=True)
                elif kind == "vx":
                    if which == 0:
                        pe.wait_ge(d_wv2, 16)
                    for c in range(KC):
                        t = (which * KC + c) * P
                        last = mm(bank[:, c * P:(c + 1) * P], ctx_t[:, t:t + P], wv2[:, :], start=True, stop=True)
                elif kind == "x_t":
                    pe.wait_ge(s_xhat, 1)
                    for c in range(NC_):
                        last = turn(bank[:, c * P:(c + 1) * P], x_hat[:, c, :], ident[:, :])
                elif kind in "qk":
                    if which == 0:
                        pe.wait_ge(d_wq1 if kind == "q" else d_wk1, 16)
                    if kind == "q" and which == 0:
                        pe.wait_ge(s_ev["act"], evacuated(index_of("x_t", 0))[1])
                    w = wq1 if kind == "q" else wk1
                    last = mm(bank, w[:, which * P:(which + 1) * P], x_hat_t[:, :], start=True, stop=True)
                else:
                    c, half = which
                    if which == (0, 0):
                        pe.wait_ge(d_wv1, 16)
                    last = mm(bank, x_hat_t[:, c * P:(c + 1) * P], wv1[:, half * BANK:(half + 1) * BANK],
                              start=True, stop=True)
                last.then_inc(s_item, 1)

            def out_proj1(b):
                if b == 0:
                    pe.wait_ge(d_wo1, 16)
                pe.wait_ge(s_o1, NP * (b + 1))
                for c in range(C):
                    t = b * S + c * P
                    for p in range(NP):
                        last = mm(ps[:, MID_BANK, c * P:(c + 1) * P], o1_t[:, p, t:t + P], wo1[:, p, :],
                                  start=p == 0, stop=p == NP - 1)
                last.then_inc(s_wo, 1)

            def out_proj2(b):
                if b == 0:
                    pe.wait_ge(d_pad, 32 * HG)
                pe.wait_ge(s_o2, NG * (b + 1))
                for c in range(C):
                    t = b * S + c * P
                    for hg in range(NG):
                        last = mm(ps[:, MID_BANK, c * P:(c + 1) * P], o2_t[:, hg, t:t + P], wo2[:, hg, :],
                                  start=hg == 0, stop=hg == NG - 1)
                last.then_inc(s_wo, 1)

            def turn_x_hat(k, b):
                pe.wait_ge(s_xhat, k + 1)
                for c in range(C):
                    last = turn(ps[:, MID_BANK, c * P:(c + 1) * P], x_hat[:, b * C + c, :], ident[:, :])
                last.then_inc(s_xhat_ps, 1)

            def query2(b):
                if b == 0:
                    pe.wait_ge(d_wq2, 16)
                pe.wait_ge(s_xhat_t, b + 1)
                mm(ps[:, MID_BANK, S:2 * S], wq2[:, :], x_hat_t[:, b * S:(b + 1) * S],
                   start=True, stop=True).then_inc(s_q2ps, 1)

            def between(what):
                kind, b = what
                if kind == "wo":
                    out_proj1(b)
                elif kind == "turn":
                    turn_x_hat(1 + b, b)
                elif kind == "q":
                    query2(b)
                elif kind == "wo2":
                    out_proj2(b)
                elif kind == "turn2":
                    turn_x_hat(3 + b, b)

            pe.wait_ge(s_ev["act"], evacuated(index_of("v", (NC_ - 1, 0)))[1])
            pe.wait_ge(s_ev["dve"], evacuated(index_of("v", (NC_ - 1, 1)))[1])
            for s in range(N_SELF + 2):
                if s < N_SELF:
                    b, p = divmod(s, NP)
                    for r in range(2):
                        if s >= 2:
                            pe.wait_ge(s_exp1, 2 * (s - 2) + r + 1)
                        rows = slice(HD1 * r, HD1 * (r + 1))
                        for c in range(C):
                            last = mm(ps[:, 2 * (s % 2) + r, c * S:(c + 1) * S],
                                      q1_t[rows, p, b * S + c * P:b * S + (c + 1) * P],
                                      k1_t[rows, p, b * S:(b + 1) * S], start=True, stop=True)
                        last.then_inc(s_score1, 1)
                if s >= 2:
                    b, p = divmod(s - 2, NP)
                    pe.wait_ge(s_pt1, 2 * (s - 1))
                    if s >= 3:
                        pe.wait_ge(s_o1, s - 2)
                    for c in range(C):
                        for r in range(2):
                            h = 2 * p + r
                            last = mm(ps[HD1 * r:HD1 * (r + 1), O_BANK, 0:S],
                                      v1[:, b * C + c, h * HD1:(h + 1) * HD1],
                                      prob1_t[:, s % 2, r, c * S:(c + 1) * S],
                                      start=c == 0, stop=c == C - 1)
                    last.then_inc(s_pv1, 1)
                if 1 <= s <= N_SELF:
                    for r in range(2):
                        pe.wait_ge(s_norm1, 2 * (s - 1) + r + 1)
                        if s >= 2:
                            pe.wait_ge(s_pt1, 2 * (s - 2) + r + 1)
                        for c in range(C):
                            for i in range(C):
                                last = turn(ps[:, PT_BANK + r, i * S + c * P:i * S + (c + 1) * P],
                                            prob1[:, (s - 1) % 2, r, c * S + i * P:c * S + (i + 1) * P], ident[:, :])
                        last.then_inc(s_turn1, 1)
                if s in SELF_MID:
                    between(SELF_MID[s])

            pe.wait_ge(d_kstack, 16 * PARTS * PARTS)
            pe.wait_ge(s_pt1, 2 * N_SELF)
            pe.wait_ge(s_o1, N_SELF)
            for n in range(N_CROSS + 3):
                if n < N_CROSS:
                    b, h = divmod(n, H2)
                    if h == 0:
                        pe.wait_ge(d_qstack[b], 16 * PARTS * PARTS)
                    for c in range(C):
                        if n >= 2:
                            pe.wait_ge(s_low2, C * (n - 2) + c + 1)
                        t = b * S + c * P
                        mm(ps[:, 2 * (n % 2) + c, :], q2_stack[:, h, t:t + P],
                           k2_stack[:, h, b * SK:(b + 1) * SK], start=True, stop=True).then_inc(s_score2, 1)
                if n % HG == 1 and n > HG:
                    k = (n - HG - 1) // HG
                    b, hg = divmod(k, NG)
                    pe.wait_ge(s_pt2a, HG * (k + 1))
                    pe.wait_ge(s_pt2b, HG * (k + 1))
                    if k >= 1:
                        pe.wait_ge(s_o2n, k)
                    for kc in range(KC):
                        for g in range(HG):
                            last = mm(ps[CW * g:CW * (g + 1), O_BANK, 0:S], v2[:, b * KC + kc, HG * hg + g, :],
                                      prob2_t[(HG * k + g) % PT_SLOTS][:, kc, :],
                                      start=kc == 0, stop=kc == KC - 1)
                    pe.wait_ge(s_wide2, k + 1)
                    for c in range(C):
                        last = turn(ps[:, O_BANK, S + c * P:S + (c + 1) * P], rec2_wide[:, k % 2, c, :], ident[:, :])
                    last.then_inc(s_rec2ps, 1)
                if 1 <= n <= N_CROSS:
                    pe.wait_ge(s_exp2, C * n)
                    for half, done, free in ((0, s_turn2a, s_pt2a), (1, s_turn2b, s_pt2b)):
                        if n >= 2:
                            pe.wait_ge(free, n - 1)
                        for k2 in range(2):
                            kc = 2 * half + k2
                            for c in range(C):
                                last = turn(ps[:, PT_BANK + half, k2 * S + c * P:k2 * S + (c + 1) * P],
                                            prob2[:, (n - 1) % 2, c, kc * P:(kc + 1) * P], ident[:, :])
                        last.then_inc(done, 1)
                if n in CROSS_MID:
                    between(CROSS_MID[n])
            out_proj2(1)
            turn_x_hat(4, 1)

            pe.wait_ge(d_ffn, 16 * 5)
            pe.wait_ge(s_xhat_t, 4)
            for c in range(NC_):
                last = mm(ps[:, O_BANK, c * NE:(c + 1) * NE], x_hat_t[:, c * P:(c + 1) * P], gate_w[:, :],
                          start=True, stop=True)
            last.then_inc(s_logit, 1)
            for k in range(NE + 2):
                if k <= NE:
                    e = (k - 1) % (NE + 1)
                    if k >= 1:
                        pe.wait_ge(s_silu, k)
                    for f in range(FC):
                        last = mm(ps[:, f, :], wg[:, e, f * P:(f + 1) * P], x_hat_t[:, :], start=True, stop=True)
                    last.then_inc(s_g, 1)
                    if k >= 1:
                        pe.wait_ge(s_hid, k)
                    for f in range(FC):
                        last = mm(ps[:, 2 + f, :], wu[:, e, f * P:(f + 1) * P], x_hat_t[:, :], start=True, stop=True)
                    last.then_inc(s_u, 1)
                if k >= 1:
                    e = (k - 2) % (NE + 1)
                    if k == 1:
                        pe.wait_ge(d_wd, 32)
                    pe.wait_ge(s_hid, k)
                    if k >= 3:
                        pe.wait_ge(s_ypart, k - 2)
                    for c in range(NC_):
                        for f in range(FC):
                            last = mm(ps[:, 4 + (k - 1) % 2, c * P:(c + 1) * P],
                                      hid[:, (k - 1) % 2, f, c * P:(c + 1) * P], wd[:, e, f, :],
                                      start=f == 0, stop=f == FC - 1)
                    last.then_inc(s_y, 1)

        @block.vector
        def _(dve):
            chain = [0]

            def link(ins):
                chain[0] += 1
                ins.then_inc(s_dve, 1)
                dve.wait_ge(s_dve, chain[0])

            def normalise(k, src, first, count):
                for c in range(first, first + count):
                    ins = nc.vector.bn_stats(stats[:, c, :], src[:, c, :])
                link(ins)
                for c in range(first, first + count):
                    ins = nc.vector.bn_aggr(mean_var[:, c, :], stats[:, c, :])
                ins.then_inc(s_var, 1)
                dve.wait_ge(s_var, k + 1)
                dve.wait_ge(s_rstd, k + 1)
                for c in range(first, first + count):
                    ins = nc.vector.tensor_scalar(x_hat[:, c, :], src[:, c, :], mean_var[:, c, 0:1],
                                                  rstd[:, c:c + 1], ALU.subtract, ALU.mult)
                ins.then_inc(s_xhat, 1)

            dve.wait_ge(d_x, 16)
            normalise(0, x_in, 0, NC_)

            def split(full, rest_, parts):
                link(nc.vector.tensor_copy(parts[:, 0, :], full))
                link(nc.vector.tensor_tensor(rest_, full, parts[:, 0, :], ALU.subtract))
                link(nc.vector.tensor_copy(parts[:, 1, :], rest_))
                return nc.vector.tensor_tensor(parts[:, 2, :], rest_, parts[:, 1, :], ALU.subtract)

            dve.wait_ge(d_bias, 16 * 5)
            for j, (kind, which, engine) in enumerate(ITEMS):
                if engine != "dve":
                    continue
                dve.wait_ge(s_item, j + 1)
                bank = ps[:, j % 8, :]
                if kind == "k":
                    ins = nc.vector.tensor_scalar(k1_t[:, which, :], bank, bias1[:, 1, which:which + 1], None, ALU.add)
                else:
                    c, half = which
                    ins = nc.vector.tensor_copy(v1[:, c, half * BANK:(half + 1) * BANK], bank)
                ins.then_inc(s_ev["dve"], 1)
                if (kind, which) == ("k", 1):
                    dve.wait_ge(s_ev["act"], evacuated(index_of("kx", 1))[1])
                    split(k2_t, k2_rest, k2_parts).then_inc(s_kparts, 1)
                if (kind, which) == ("k", 4):
                    dve.wait_ge(d_mask, 16)
                    nc.vector.tensor_scalar(mask_add[:, :, :], mask_in, 0, MASKED, ALU.is_equal, ALU.mult
                                            ).then_inc(s_maskadd, 1)

            def residual(k, b, dst, src, done):
                dve.wait_ge(s_wo, k + 1)
                ins = nc.vector.tensor_tensor(dst[:, b * C:(b + 1) * C, :],
                                              ps[:, MID_BANK, 0:C * P].rearrange("p (c n) -> p c n", c=C),
                                              src[:, b * C:(b + 1) * C, :], ALU.add)
                ins.then_inc(done, 1)
                dve.wait_ge(done, b + 1)

            def between(what):
                kind, b = what
                if kind == "wo":
                    dve.wait_ge(s_xbo, C * (b + 1))
                    residual(b, b, x1, x_bo, s_x1)
                    normalise(1 + b, x1, b * C, C)
                elif kind == "q":
                    dve.wait_ge(s_q2ps, b + 1)
                    if b >= 1:
                        dve.wait_ge(d_qdram[b - 1], 16)
                    link(nc.vector.tensor_scalar(q2_t[:, :], ps[:, MID_BANK, S:2 * S], bias2[:, 0:1], -SCALE2,
                                                 ALU.add, ALU.mult))
                    split(q2_t[:, :], q2_rest[:, :], q2_parts).then_inc(s_qparts, 1)
                elif kind == "wo2":
                    dve.wait_ge(s_x1bo, C * (b + 1))
                    residual(2 + b, b, x2, x1_bo, s_x2)
                    normalise(3 + b, x2, b * C, C)

            for s in range(N_SELF + 2):
                if 1 <= s <= N_SELF:
                    for r in range(2):
                        dve.wait_ge(s_exp1, 2 * (s - 1) + r + 1)
                        nc.vector.reciprocal(rec1[:, (s - 1) % 2, r, :], sum1[:, (s - 1) % 2, r, :]
                                             ).then_inc(s_rec1, 1)
                if s < N_SELF:
                    for r in range(2):
                        dve.wait_ge(s_score1, 2 * s + r + 1)
                        nc.vector.tensor_reduce(low1[:, s % 2, r, :],
                                                ps[:, 2 * (s % 2) + r, :].rearrange("p (c i) -> p c i", c=C),
                                                AX.X, ALU.min).then_inc(s_low1, 1)
                if 1 <= s <= N_SELF:
                    for r in range(2):
                        dve.wait_ge(s_turn1, 2 * (s - 1) + r + 1)
                        nc.vector.tensor_copy(prob1_t[:, (s - 1) % 2, r, :], ps[:, PT_BANK + r, :]
                                              ).then_inc(s_pt1, 1)
                if s in SELF_MID:
                    between(SELF_MID[s])

            dve.wait_ge(s_maskadd, 1)
            for n in range(N_CROSS + 3):
                if n < N_CROSS:
                    for c in range(C):
                        dve.wait_ge(s_score2, C * n + c + 1)
                        if n >= 2:
                            dve.wait_ge(s_exp2, C * (n - 2) + c + 1)
                        nc.vector.tensor_tensor_reduce(out=score2[:, n % 2, c, :], in0=ps[:, 2 * (n % 2) + c, :],
                                                       in1=mask_add[:, c, :], scale=1.0, scalar=3e38,
                                                       op0=ALU.add, op1=ALU.min, accum_out=low2[:, n % 2, c:c + 1]
                                                       ).then_inc(s_low2, 1)
                if n % HG == 0 and n >= HG:
                    k = n // HG - 1
                    dve.wait_ge(s_exp2, C * n)
                    nc.vector.reciprocal(rec2[:, k % 2, :, :], sum2[:, k % 2, :, :]).then_inc(s_rec2, 1)
                if 1 <= n <= N_CROSS:
                    dve.wait_ge(s_turn2a, n)
                    nc.vector.tensor_copy(prob2_t[(n - 1) % PT_SLOTS][:, 0:2, :],
                                          ps[:, PT_BANK, :].rearrange("p (k t) -> p k t", k=2)).then_inc(s_pt2a, 1)
                if n % HG == 2 and n > HG:
                    k = (n - HG - 2) // HG
                    b, hg = divmod(k, NG)
                    dve.wait_ge(s_rec2t, k + 1)
                    nc.vector.tensor_tensor(o2_t[:, hg, b * S:(b + 1) * S], ps[:, O_BANK, 0:S], rec2_t[:, :],
                                            ALU.mult).then_inc(s_o2n, 1)
                if n in CROSS_MID:
                    between(CROSS_MID[n])
            between(("wo2", 1))

            def wide(i):
                return col[:, i, :].unsqueeze(2).to_broadcast([P, NC_, NE])

            v = nc.vector
            dve.wait_ge(s_logit, 1)
            link(v.tensor_copy(logit[:, :, :], ps[:, O_BANK, 0:NC_ * NE].rearrange("p (c e) -> p c e", c=NC_)))
            link(v.tensor_reduce(col[:, 0, :], logit[:, :, :], AX.X, ALU.max))
            v.tensor_tensor(logit[:, :, :], logit[:, :, :], wide(0), ALU.subtract).then_inc(s_lshift, 1)

            def hidden(k):
                dve.wait_ge(s_silu, k + 1)
                dve.wait_ge(s_u, k + 1)
                if k >= 2:
                    dve.wait_ge(s_y, k - 1)
                v.tensor_tensor(hid[:, k % 2], silu[:, k % 2, :].rearrange("p (f t) -> p f t", f=FC),
                                ps[:, 2:4, :], ALU.mult).then_inc(s_hid, 1)

            def gate_weights():
                dve.wait_ge(s_gexp, 1)
                dve.wait_ge(s_const, 1 + NE)
                link(v.tensor_reduce(col[:, 1, :], gate_e[:, :, :], AX.X, ALU.add))
                link(v.reciprocal(col[:, 2, :], col[:, 1, :]))
                link(v.tensor_tensor(gate_s[:, :, :], gate_e[:, :, :], wide(2), ALU.mult))

                def first_largest(values, to):
                    link(v.tensor_reduce(col[:, 3, :], values, AX.X, ALU.max))
                    link(v.tensor_tensor(pick[:, :, :], values, wide(3), ALU.is_equal))
                    link(v.tensor_tensor(pick[:, :, :], pick[:, :, :], rank[:, :, :], ALU.mult))
                    link(v.tensor_reduce(col[:, 4, :], pick[:, :, :], AX.X, ALU.max))
                    link(v.tensor_tensor(to, pick[:, :, :], wide(4), ALU.is_equal))

                first_largest(gate_s[:, :, :], pick1[:, :, :])
                link(v.scalar_tensor_tensor(out=rest[:, :, :], in0=pick1[:, :, :], scalar=-2.0, in1=gate_s[:, :, :],
                                            op0=ALU.mult, op1=ALU.add))
                first_largest(rest[:, :, :], pick2[:, :, :])
                link(v.tensor_tensor(pick[:, :, :], pick1[:, :, :], pick2[:, :, :], ALU.add))
                link(v.tensor_tensor(pick[:, :, :], pick[:, :, :], gate_s[:, :, :], ALU.mult))
                link(v.tensor_reduce(col[:, 5, :], pick[:, :, :], AX.X, ALU.add))
                link(v.tensor_scalar(col[:, 5, :], col[:, 5, :], 1e-20, None, ALU.add))
                link(v.reciprocal(col[:, 0, :], col[:, 5, :]))
                v.tensor_tensor(w_e[:, :, :], pick[:, :, :], wide(0), ALU.mult).then_inc(s_we, 1)
                dve.wait_ge(s_we, 1)

            def bank_y(k):
                return ps[:, 4 + k % 2, :].rearrange("p (c n) -> p c n", c=NC_)

            hidden(0)
            gate_weights()
            hidden(1)
            for k in range(NE):
                dve.wait_ge(s_y, k + 1)
                if k == 0:
                    v.tensor_tensor(acc, bank_y(0), x2[:, :, :], ALU.add).then_inc(s_ypart, 1)
                else:
                    if k >= 3:
                        dve.wait_ge(s_acc, k - 2)
                    v.tensor_tensor(y_part[:, k % 2], bank_y(k),
                                    w_e[:, :, k - 1:k].to_broadcast([P, NC_, D]), ALU.mult).then_inc(s_ypart, 1)
                if k + 2 <= NE:
                    hidden(k + 2)
            dve.wait_ge(s_y, NE + 1)
            dve.wait_ge(s_acc, NE - 1)
            for c in range(NC_):
                v.scalar_tensor_tensor(out=y_out[:, c, :], in0=bank_y(NE)[:, c, :], scalar=w_e[:, c, NE - 1:NE],
                                       in1=acc[:, c, :], op0=ALU.mult, op1=ALU.add).then_inc(s_out, 1)


INPUTS = ["x", "ctx_1024", "mask_1x1xSxS2_ik1"]
INPUTS += [f"L0_{part}_{w}{k}" for part in ("attn", "xattn") for k in "qkvo" for w in ("W", "b")]
INPUTS += ["L0_ffn_" + w for w in ("gate_w", "w_gate", "w_up", "w_down", "ws_gate", "ws_up", "ws_down")]


def kernel(**inputs):
    import numpy as np
    import concourse.bacc as bacc
    from concourse.bass_utils import run_bass_kernel_spmd

    nc = bacc.Bacc("TRN2", target_bir_lowering=False, num_devices=1)
    arrays, aps = {}, {}
    for name in INPUTS:
        array = np.asarray(inputs[name])
        if name in ("L0_attn_bq", "L0_attn_bk", "L0_attn_bv"):
            array = array.reshape(NP, P).T
        if name == "L0_xattn_bv":
            array = array.reshape(NG, HG, HD2).transpose(1, 2, 0)
        array = np.ascontiguousarray(array)
        arrays[f"in_{name}"] = array
        aps[name] = nc.dram_tensor(f"in_{name}", array.shape, mybir.dt.from_np(array.dtype), kind="ExternalInput").ap()
    out = nc.dram_tensor("out", (B, S, D), F32, kind="ExternalOutput").ap()
    build(nc, aps, out)
    return run_bass_kernel_spmd(nc, [arrays], core_ids=[0]).results[0]["out"]
```

```python
from contextlib import ExitStack

import concourse.bass as bass
from concourse import mybir

F32 = mybir.dt.float32
BF16 = mybir.dt.bfloat16
ALU = mybir.AluOpType
ACT = mybir.ActivationFunctionType
AX = mybir.AxisListType

P = 128
B, S, D = 2, 256, 128
C = S // P
NC_ = B * C
T = B * S
H1, HD1 = 16, 64
NP = H1 // 2
H2, HD2 = 16, 8
SK = 512
KC = SK // P
TK = B * SK
PARTS = 3
KSTACK = PARTS * PARTS * HD2
HG = 4
NG = H2 // HG
CW = P // HG
NE, FF = 8, 256
FC = FF // P
EPS = 1e-5
MASKED = 1e30
BANK = 512
SCALE1 = 1.0 / 8.0
SCALE2 = float(HD2) ** -0.5
PT_SLOTS = 6
WARM_UP = 8

PT_BANK, O_BANK, MID_BANK = 4, 6, 7

N_SELF = B * NP
N_CROSS = B * H2
LAG_T, LAG_V = 2, 3
LAST_G = N_SELF + N_CROSS + LAG_V + 2
BETWEEN = {
    11: [("wo", 0, 0), ("wo", 0, 1), ("residual", 0, 0)],
    12: [("x_hat", 0, 0), ("turn", 0, 0), ("turned", 0, 0)],
    13: [("q", 0, 0), ("parts", 0, 0)],
    N_SELF + 3: [("wo", 1, 0)],
    N_SELF + 4: [("wo", 1, 1)],
    N_SELF + 5: [("residual", 1, 0)],
    N_SELF + 6: [("x_hat", 1, 0)],
    N_SELF + 7: [("turn", 1, 0)],
    N_SELF + 8: [("turned", 1, 0)],
    N_SELF + 9: [("q", 1, 0)],
    N_SELF + 10: [("parts", 1, 0)],
    N_SELF + 25: [("wo2", 0, 0)],
    N_SELF + 26: [("residual2", 0, 0)],
    N_SELF + 27: [("x_hat2", 0, 0)],
    N_SELF + 28: [("turn2", 0, 0)],
    N_SELF + 29: [("turned2", 0, 0)],
    N_SELF + 30: [("gate", 0, 0)],
    N_SELF + 31: [("shift", 0, 0)],
    N_SELF + 32: [("gate_exp", 0, 0)],
}
N_FFN = B * (NE + 1)
FFN_BETWEEN = {
    0: [("wo2", 1, 0), ("residual2", 1, 0)],
    1: [("x_hat2", 1, 0), ("weights", 0, 0)],
    2: [("turn2", 1, 0), ("turned2", 1, 0)],
    3: [("gate", 1, 0)],
    4: [("shift", 1, 0), ("gate_exp", 1, 0)],
    6: [("weights", 1, 0)],
}


def items():
    out = [("ctx_t", 0, "act"), ("ctx_t", 1, "act"), ("kx", 0, "act"), ("x_t", 0, "dve"), ("kx", 1, "act")]
    for p in range(NP):
        if p == 2:
            out += [("vx", 0, "act"), ("vx", 1, "act")]
        out += [("q", p, "act"), ("k", p, "dve")]
    return out


ITEMS = items()
V_BANKS = (7, 4, 5, 6)
V_ITEMS = {g: [(c, half) for c in (2 * g, 2 * g + 1) for half in (0, 1)] for g in range(NC_ // 2)}


def evacuated(j):
    engine = ITEMS[j][2]
    return engine, sum(1 for x in ITEMS[:j + 1] if x[2] == engine)


def index_of(kind, which):
    return [x[:2] for x in ITEMS].index((kind, which))


def build(nc, a, out):
    with ExitStack() as ctx:
        def sb(name, shape, dt=F32):
            return ctx.enter_context(nc.sbuf_tensor(name, shape, dt))

        def sem(name):
            return ctx.enter_context(nc.semaphore(name))

        ps = ctx.enter_context(nc.psum_tensor("ps", [P, 8, BANK], F32))

        ident = sb("ident", [P, P])
        x_in = sb("x_in", [P, NC_, D])
        x_bo = sb("x_bo", [P, NC_, D])
        x1 = sb("x1", [P, NC_, D])
        x1_bo = x_bo
        x2 = x_in
        bo1 = sb("bo1", [P, D])
        bo2 = sb("bo2", [P, D])
        stats = sb("stats", [P, NC_, 6])
        mean_var = sb("mean_var", [P, NC_, 2])
        var_eps = sb("var_eps", [P, NC_])
        minus_half = sb("minus_half", [P, NC_])
        rstd = sb("rstd", [P, NC_])
        x_hat = sb("x_hat", [P, NC_, D])
        x_hat_t = sb("x_hat_t", [P, T])
        w_in1 = sb("w_in1", [P, 3, H1 * HD1])
        wq1, wk1, wv1 = (w_in1[:, i, :] for i in range(3))
        wo1 = sb("wo1", [P, NP, D])
        biases = sb("biases", [P, 3 * NP + 2])
        bias1 = biases[:, 0:3 * NP].rearrange("p (i n) -> p i n", i=3)
        bias2 = biases[:, 3 * NP:3 * NP + 2]
        bq1_s = sb("bq1_s", [P, NP])
        q1_t = sb("q1_t", [P, NP, T])
        k1_t = sb("k1_t", [P, NP, T])
        v1 = sb("v1", [P, NC_, H1 * HD1])
        o1_t = sb("o1_t", [P, NP, T])
        low1 = sb("low1", [P, 2, 2, C])
        sum1 = sb("sum1", [P, 2, 2, C])
        rec1 = sb("rec1", [P, 2, 2, C])
        prob1 = sb("prob1", [P, 3, 2, C * S])
        prob1_t = sb("prob1_t", [P, 2, 2, C * S])
        prob1_flat = prob1[:, :, :, :].rearrange("p a r n -> p (a r n)")
        prob1_t_flat = prob1_t[:, :, :, :].rearrange("p a r n -> p (a r n)")

        k2_parts = prob1_flat[:, 0:PARTS * TK // 2].bitcast(BF16).rearrange("p (j t) -> p j t", j=PARTS)
        mask_in = prob1_t_flat[:, 0:C * SK].bitcast(mybir.dt.int32).rearrange("p (c k) -> p c k", c=C)
        ctx_in = prob1_t_flat[:, C * SK:C * SK + B * KC * D].rearrange("p (c d) -> p c d", d=D)
        context = sb("context", [P, 3, TK])
        ctx_t, k2_t, k2_rest = (context[:, i, :] for i in range(3))
        wq2 = sb("wq2", [P, D])
        wk2 = sb("wk2", [P, D])
        wv2 = sb("wv2", [P, D])
        wo2 = sb("wo2", [P, NG, D])
        bv2 = sb("bv2", [P, NG])
        mask_add = sb("mask_add", [P, C, SK])
        q2_t = sb("q2_t", [P, S])
        q2_rest = sb("q2_rest", [P, S])
        q2_parts = sb("q2_parts", [P, PARTS, S], BF16)
        k2_stack = sb("k2_stack", [KSTACK, H2, TK], BF16)
        q2_stack = sb("q2_stack", [KSTACK, H2, T], BF16)
        v2 = sb("v2", [P, B * KC, H2, CW])
        low2 = sb("low2", [P, 2, C])
        sum2 = sb("sum2", [P, 2, C, HG])
        rec2 = sb("rec2", [P, 2, C, HG])
        rec2_wide = sb("rec2_wide", [P, 2, C, P])
        o_rec = sb("o_rec", [P, 2, S])
        def attn_tile(t, i):
            return t[:, 2 * i:2 * i + 2, :].rearrange("p a n -> p (a n)")

        score2 = [attn_tile(q1_t, i).rearrange("p (c k) -> p c k", c=C) for i in (0, 1)]
        prob2 = [attn_tile(*x).rearrange("p (c k) -> p c k", c=C) for x in ((q1_t, 2), (q1_t, 3), (k1_t, 0))]
        prob2_t = [attn_tile(k1_t, 1)]
        prob2_t += [prob1_flat[:, i * KC * S:(i + 1) * KC * S] for i in range(3)]
        prob2_t += [prob1_t_flat[:, i * KC * S:(i + 1) * KC * S] for i in range(2)]
        prob2_t = [x.rearrange("p (k t) -> p k t", t=S) for x in prob2_t]
        o2_t = k1_t[:, 4:8, :]

        gate_w = sb("gate_w", [P, NE])
        wg, wu = (t[:, :, :].rearrange("p a n -> p (a n)")[:, 0:(NE + 1) * FF].rearrange("p (e f) -> p e f", f=FF)
                  for t in (w_in1, context))
        wd = v1[:, :, :].rearrange("p c n -> p (c n)")[:, 0:(NE + 1) * FC * D]\
            .rearrange("p (e f n) -> p e f n", e=NE + 1, f=FC)
        silu = [q1_t[:, i, :] for i in (0, 1)]
        hid = [q1_t[:, i, :].rearrange("p (f t) -> p f t", f=FC) for i in (2, 3)]
        y_part = [k1_t[:, 2 + i, 0:C * D].rearrange("p (c n) -> p c n", c=C) for i in (0, 1)]
        acc = k1_t[:, 0, :].rearrange("p (c n) -> p c n", c=NC_)
        y_out = k1_t[:, 1, :].rearrange("p (c n) -> p c n", c=NC_)
        rank = sb("rank", [P, NC_, NE])
        logit = sb("logit", [P, NC_, NE])
        gate_e = sb("gate_e", [P, NC_, NE])
        gate_s = sb("gate_s", [P, NC_, NE])
        pick = sb("pick", [P, NC_, NE])
        pick1 = sb("pick1", [P, NC_, NE])
        pick2 = sb("pick2", [P, NC_, NE])
        rest = sb("rest", [P, NC_, NE])
        w_e = sb("w_e", [P, NC_, NE])
        col = sb("col", [P, 6, NC_])

        k2_dram = nc.dram_tensor("k2_dram", [PARTS, D, TK], BF16, kind="Internal").ap()
        q2_dram = nc.dram_tensor("q2_dram", [B, PARTS, D, S], BF16, kind="Internal").ap()

        d_x, d_wk2, d_wv2, d_wq2 = map(sem, ("d_x", "d_wk2", "d_wv2", "d_wq2"))
        d_ctx = [sem(f"d_ctx{b}") for b in range(B)]
        d_wq1, d_wk1, d_wv1, d_wo1 = map(sem, ("d_wq1", "d_wk1", "d_wv1", "d_wo1"))
        d_bias, d_mask, d_bo, d_pad, d_ffn, d_wd = map(sem, ("d_bias", "d_mask", "d_bo", "d_pad", "d_ffn", "d_wd"))
        d_kdram, d_kstack, d_out = map(sem, ("d_kdram", "d_kstack", "d_out"))
        d_qdram = [sem(f"d_qdram{b}") for b in range(B)]
        d_qstack = [sem(f"d_qstack{b}") for b in range(B)]
        s_pad0, s_const, s_ident = map(sem, ("s_pad0", "s_const", "s_ident"))
        s_dve, s_pool = map(sem, ("s_dve", "s_pool"))
        s_v = sem("s_v")
        s_vev = {0: sem("s_vev_act"), 1: sem("s_vev_dve")}
        s_item = sem("s_item")
        s_ev = {"act": sem("s_ev_act"), "dve": sem("s_ev_dve")}
        s_bq = sem("s_bq")
        s_var, s_rstd, s_xhat, s_xhat_ps, s_xhat_t = map(sem, ("s_var", "s_rstd", "s_xhat", "s_xhat_ps", "s_xhat_t"))
        s_kparts, s_qparts, s_maskadd = map(sem, ("s_kparts", "s_qparts", "s_maskadd"))
        s_xbo, s_x1, s_x1bo, s_x2 = map(sem, ("s_xbo", "s_x1", "s_x1bo", "s_x2"))
        s_score1, s_low1, s_exp1, s_rec1, s_norm1 = map(sem, ("s_score1", "s_low1", "s_exp1", "s_rec1", "s_norm1"))
        s_turn1, s_pt1, s_pv1, s_o1 = map(sem, ("s_turn1", "s_pt1", "s_pv1", "s_o1"))
        s_wo, s_q2ps = map(sem, ("s_wo", "s_q2ps"))
        s_wide2 = sem("s_wide2")
        s_score2, s_low2, s_exp2, s_rec2 = map(sem, ("s_score2", "s_low2", "s_exp2", "s_rec2"))
        s_turn2a, s_turn2b, s_pt2a, s_pt2b = map(sem, ("s_turn2a", "s_turn2b", "s_pt2a", "s_pt2b"))
        s_orec_ps, s_orec, s_o2 = map(sem, ("s_orec_ps", "s_orec", "s_o2"))
        s_logit, s_lshift, s_gexp, s_we = map(sem, ("s_logit", "s_lshift", "s_gexp", "s_we"))
        s_g, s_u, s_silu, s_hid, s_y, s_ypart, s_acc = map(sem, (
            "s_g", "s_u", "s_silu", "s_hid", "s_y", "s_ypart", "s_acc"))

        def chunks(ap):
            return ap.rearrange("b (c p) d -> p (b c) d", p=P)

        block = ctx.enter_context(nc.Block())

        @block.sync
        def _(sp):
            def load(dst, src, s):
                sp.dma_start(dst, src).then_inc(s, 16)

            load(x_in[:, :, :], chunks(a["x"]), d_x)
            for b in range(B):
                load(ctx_in[:, b * KC:(b + 1) * KC, :], chunks(a["ctx_1024"])[:, b * KC:(b + 1) * KC, :], d_ctx[b])
            load(wk2[:, :], a["L0_xattn_Wk"], d_wk2)
            load(wq1, a["L0_attn_Wq"], d_wq1)
            load(wk1, a["L0_attn_Wk"], d_wk1)
            load(wv2[:, :], a["L0_xattn_Wv"], d_wv2)
            load(wv1, a["L0_attn_Wv"], d_wv1)
            load(mask_in, a["mask_1x1xSxS2_ik1"].rearrange("a b (c p) k -> p (a b c) k", p=P), d_mask)
            load(wq2[:, :], a["L0_xattn_Wq"], d_wq2)
            load(wo1[:, :, :], a["L0_attn_Wo"].rearrange("(p r) n -> r p n", r=P), d_wo1)
            sp.wait_ge(s_kparts, 1)
            load(k2_dram.rearrange("j r t -> r j t"), k2_parts, d_kdram)
            sp.wait_ge(d_kdram, 16)
            for j in range(PARTS):
                for i in range(PARTS):
                    r = (j * PARTS + i) * HD2
                    load(k2_stack[r:r + HD2, :, :], k2_dram[j].rearrange("(d h) t -> d h t", d=HD2), d_kstack)
            sp.wait_ge(s_v, NC_ * 2)
            load(wg[:, 0:NE, :], a["L0_ffn_w_gate"].rearrange("e d f -> d e f"), d_ffn)
            load(wu[:, 0:NE, :], a["L0_ffn_w_up"].rearrange("e d f -> d e f"), d_ffn)
            load(wg[:, NE, :], a["L0_ffn_ws_gate"], d_ffn)
            load(wu[:, NE, :], a["L0_ffn_ws_up"], d_ffn)
            load(gate_w[:, :], a["L0_ffn_gate_w"], d_ffn)
            for b in range(B):
                sp.wait_ge(s_qparts, b + 1)
                load(q2_dram[b].rearrange("i r t -> r i t"), q2_parts[:, :, :], d_qdram[b])
                sp.wait_ge(d_qdram[b], 16)
                for j in range(PARTS):
                    r = j * PARTS * HD2
                    load(q2_stack[r:r + PARTS * HD2, :, b * S:(b + 1) * S],
                         q2_dram[b].rearrange("i (d h) t -> (i d) h t", d=HD2), d_qstack[b])
                if b == 0:
                    sp.wait_ge(s_pv1, N_SELF)
                    load(wd[:, 0:NE, :, :], a["L0_ffn_w_down"].rearrange("e (f r) n -> r e f n", r=P), d_wd)
                    load(wd[:, NE, :, :], a["L0_ffn_ws_down"].rearrange("(f r) n -> r f n", r=P), d_wd)
            out_c = chunks(out)
            for b in range(B):
                sp.wait_ge(s_ypart, (b + 1) * (NE + 1))
                load(out_c[:, b * C:(b + 1) * C, :], y_out[:, b * C:(b + 1) * C, :], d_out)
            sp.wait_ge(d_out, 16 * B)

        @block.gpsimd
        def _(pool):
            chain = [0]

            def link(ins):
                chain[0] += 1
                ins.then_inc(s_pool, 1)
                pool.wait_ge(s_pool, chain[0])

            link(nc.gpsimd.memset(ident[:, :], 0.0))
            nc.gpsimd.affine_select(out=ident[:, :], in_=ident[:, :], compare_op=ALU.not_equal, fill=1.0,
                                    base=0, pattern=[[-1, P]], channel_multiplier=1).then_inc(s_ident, 1)
            link(nc.gpsimd.memset(minus_half[:, :], -0.5))

            def reciprocal_std(k, first, count):
                pool.wait_ge(s_var, k + 1)
                link(nc.gpsimd.tensor_scalar(var_eps[:, first:first + count], mean_var[:, first:first + count, 1],
                                             EPS, None, ALU.add))
                nc.gpsimd.tensor_tensor(rstd[:, first:first + count], var_eps[:, first:first + count],
                                        minus_half[:, first:first + count], ALU.pow).then_inc(s_rstd, 1)

            reciprocal_std(0, 0, NC_)
            nc.gpsimd.memset(wo2[:, :, :], 0.0).then_inc(s_pad0, 1)
            nc.gpsimd.memset(bv2[:, :], 0.0).then_inc(s_pad0, 1)
            nc.gpsimd.memset(v2[:, :, :, :], 0.0).then_inc(s_const, 1)
            for e in range(NE):
                nc.gpsimd.memset(rank[:, :, e], float(NE - e)).then_inc(s_const, 1)
            pool.dma_start(bo1[:, :], a["L0_attn_bo"].rearrange("(o n) -> o n", o=1).to_broadcast([P, D])).then_inc(d_bo, 16)
            pool.dma_start(bo2[:, :], a["L0_xattn_bo"].rearrange("(o n) -> o n", o=1).to_broadcast([P, D])).then_inc(d_bo, 16)
            pool.wait_ge(s_pad0, 2)
            for g in range(HG):
                rows = slice(CW * g, CW * g + HD2)
                pool.dma_start(wo2[rows, :, :], a["L0_xattn_Wo"].rearrange("(k g d) n -> g d k n", g=HG, d=HD2)[g]
                               ).then_inc(d_pad, 16)
                pool.dma_start(bv2[rows, :], a["L0_xattn_bv"][g]
                               ).then_inc(d_pad, 16)
            pool.wait_ge(d_x, 16)
            pool.wait_ge(d_bo, 32)
            for c in range(NC_):
                nc.gpsimd.tensor_tensor(x_bo[:, c, :], x_in[:, c, :], bo1[:, :], ALU.add).then_inc(s_xbo, 1)

            def add_bo2(b):
                pool.wait_ge(s_x1, b + 1)
                for c in range(b * C, (b + 1) * C):
                    nc.gpsimd.tensor_tensor(x1_bo[:, c, :], x1[:, c, :], bo2[:, :], ALU.add).then_inc(s_x1bo, 1)

            def divide1(s):
                for r in range(2):
                    pool.wait_ge(s_rec1, 2 * s + r + 1)
                    pr = prob1[:, s % 3, r, :].rearrange("p (c i) -> p c i", c=C)
                    nc.gpsimd.tensor_tensor(pr, pr, rec1[:, s % 2, r, :].unsqueeze(2).to_broadcast([P, C, S]),
                                            ALU.mult).then_inc(s_norm1, 1)

            def widen(k):
                pool.wait_ge(s_rec2, k + 1)
                if k >= 2:
                    pool.wait_ge(s_orec_ps, k - 1)
                nc.gpsimd.tensor_copy(rec2_wide[:, k % 2, :, :].rearrange("p c (g d) -> p c g d", g=HG),
                                      rec2[:, k % 2, :, :].unsqueeze(3).to_broadcast([P, C, HG, CW])
                                      ).then_inc(s_wide2, 1)

            def divide2(k):
                b, hg = divmod(k, NG)
                pool.wait_ge(s_orec, k + 1)
                o = o2_t[:, hg, b * S:(b + 1) * S]
                link(nc.gpsimd.tensor_tensor(o, o_rec[:, 0, :], o_rec[:, 1, :], ALU.mult))
                nc.gpsimd.tensor_scalar(o, o, bv2[:, hg:hg + 1], None, ALU.add).then_inc(s_o2, 1)

            pool.wait_ge(d_pad, 32 * HG)
            for g in range(LAST_G + 2):
                n = g - N_SELF
                if n >= HG and n % HG == 0 and n <= N_CROSS:
                    widen(n // HG - 1)
                if 1 <= g <= N_SELF:
                    divide1(g - 1)
                for kind, b, _ in BETWEEN.get(g, ()):
                    if kind == "residual":
                        reciprocal_std(1 + b, b * C, C)
                        add_bo2(b)
                    elif kind == "residual2":
                        reciprocal_std(3 + b, b * C, C)
                if n >= 2 * HG and n % HG == 0 and n <= N_CROSS + HG:
                    divide2(n // HG - 2)
            reciprocal_std(4, C, C)
            for i in range(N_FFN):
                b, k = divmod(i, NE + 1)
                if 1 <= k < NE:
                    pool.wait_ge(s_ypart, i + 1)
                    if k > 1:
                        pool.wait_ge(s_acc, b * (NE - 1) + k - 1)
                    sums = acc[:, b * C:(b + 1) * C, :]
                    nc.gpsimd.tensor_tensor(sums, sums, y_part[k % 2], ALU.add).then_inc(s_acc, 1)

        @block.scalar
        def _(act):
            act.dma_start(biases[:, :], a["biases"]).then_inc(d_bias, 16)
            act.wait_ge(d_bias, 16)
            nc.scalar.mul(bq1_s[:, :], bias1[:, 0, :], -SCALE1).then_inc(s_bq, 1)

            def evacuate(j, kind, which):
                act.wait_ge(s_item, j + 1)
                bank = ps[:, j % 8, :]
                if kind == "ctx_t":
                    ins = nc.scalar.copy(ctx_t[:, which * BANK:(which + 1) * BANK], bank)
                elif kind == "kx":
                    ins = nc.scalar.activation(k2_t[:, which * BANK:(which + 1) * BANK], bank, ACT.Identity,
                                               bias=bias2[:, 1:2])
                elif kind == "vx":
                    if which == 0:
                        act.wait_ge(s_const, 1 + NE)
                    ins = nc.scalar.copy(v2[:, which * KC:(which + 1) * KC, :, 0:HD2],
                                         bank.rearrange("p (c h d) -> p c h d", c=KC, h=H2))
                elif kind == "q":
                    if which == 0:
                        act.wait_ge(s_bq, 1)
                    ins = nc.scalar.activation(q1_t[:, which, :], bank, ACT.Identity,
                                               bias=bq1_s[:, which:which + 1], scale=-SCALE1)
                ins.then_inc(s_ev["act"], 1)

            for j, (kind, which, engine) in enumerate(ITEMS):
                if engine == "act":
                    evacuate(j, kind, which)

            def x_hat_evac(k, b):
                act.wait_ge(s_xhat_ps, k)
                nc.scalar.copy(x_hat_t[:, b * S:(b + 1) * S], ps[:, MID_BANK, 0:S]).then_inc(s_xhat_t, 1)

            act.wait_ge(d_kdram, 16)
            def between(what):
                kind, b, _ = what
                if kind == "turned":
                    x_hat_evac(1 + b, b)
                elif kind == "turned2":
                    x_hat_evac(3 + b, b)
                elif kind == "gate_exp":
                    act.wait_ge(s_lshift, b + 1)
                    nc.scalar.activation(gate_e[:, b * C:(b + 1) * C, :], logit[:, b * C:(b + 1) * C, :], ACT.Exp
                                         ).then_inc(s_gexp, 1)

            def exp1(s):
                for r in range(2):
                    act.wait_ge(s_low1, 2 * s + r + 1)
                    if s >= 2:
                        act.wait_ge(s_rec1, 2 * (s - 2) + r + 1)
                    if s >= 3:
                        act.wait_ge(s_turn1, 2 * (s - 3) + r + 1)
                    for c in range(C):
                        e = nc.scalar.activation(prob1[:, s % 3, r, c * S:(c + 1) * S],
                                                 ps[:, 2 * (s % 2) + r, c * S:(c + 1) * S], ACT.Exp,
                                                 bias=low1[:, s % 2, r, c:c + 1], scale=-1.0,
                                                 accum_out=sum1[:, s % 2, r, c:c + 1])
                    e.then_inc(s_exp1, 1)

            def exp2(n):
                for c in range(C):
                    act.wait_ge(s_low2, C * n + c + 1)
                    if n >= 3 and c == 0:
                        act.wait_ge(s_turn2b, n - 2)
                    if n % HG == 0 and c == 0 and n >= 2 * HG:
                        act.wait_ge(s_rec2, n // HG - 1)
                    nc.scalar.activation(prob2[n % 3][:, c, :], score2[n % 2][:, c, :], ACT.Exp,
                                         bias=low2[:, n % 2, c:c + 1], scale=-1.0,
                                         accum_out=sum2[:, n // HG % 2, c, n % HG:n % HG + 1]
                                         ).then_inc(s_exp2, 1)

            for g in range(LAST_G + 2):
                n = g - N_SELF
                for i, (c, half) in enumerate(V_ITEMS.get(g, ())):
                    if half == 0:
                        act.wait_ge(s_v, len(V_BANKS) * g + i + 1)
                        nc.scalar.copy(v1[:, c, 0:BANK], ps[:, V_BANKS[i], :]).then_inc(s_vev[0], 1)
                for what in BETWEEN.get(g, ()):
                    between(what)
                if g < N_SELF:
                    exp1(g)
                if 0 <= n < N_CROSS:
                    exp2(n)
                if 0 <= g - LAG_V < N_SELF:
                    b, p = divmod(g - LAG_V, NP)
                    act.wait_ge(s_pv1, g - LAG_V + 1)
                    nc.scalar.activation(o1_t[:, p, b * S:(b + 1) * S], ps[:, O_BANK, 0:S], ACT.Identity,
                                         bias=bias1[:, 2, p:p + 1]).then_inc(s_o1, 1)
                if 0 <= n - LAG_T < N_CROSS:
                    act.wait_ge(s_turn2b, n - LAG_T + 1)
                    nc.scalar.copy(prob2_t[(n - LAG_T) % PT_SLOTS][:, 2:4, :],
                                   ps[:, PT_BANK + 1, :].rearrange("p (k t) -> p k t", k=2)).then_inc(s_pt2b, 1)
                if n >= 2 * HG and n % HG == 0:
                    k = n // HG - 2
                    act.wait_ge(s_orec_ps, k + 1)
                    if k >= 1:
                        act.wait_ge(s_o2, k)
                    nc.scalar.copy(o_rec[:, :, :], ps[:, O_BANK, :].rearrange("p (a t) -> p a t", a=2)
                                   ).then_inc(s_orec, 1)

            for i in range(N_FFN):
                act.wait_ge(s_g, i + 1)
                if i >= 2:
                    act.wait_ge(s_hid, i - 1)
                nc.scalar.activation(silu[i % 2], ps[:, i % 2, :], ACT.Silu).then_inc(s_silu, 1)
                for what in FFN_BETWEEN.get(i, ()):
                    between(what)

        @block.tensor
        def _(pe):
            mm, turn = nc.tensor.matmul, nc.tensor.transpose
            pe.wait_ge(s_ident, 1)
            for _ in range(WARM_UP):
                mm(ps[:, MID_BANK, 0:P], ident[:, :], ident[:, :], start=True, stop=True)
            for j, (kind, which, _) in enumerate(ITEMS):
                bank = ps[:, j % 8, :]
                if j >= 8:
                    engine, value = evacuated(j - 8)
                    pe.wait_ge(s_ev[engine], value)
                if kind == "ctx_t":
                    pe.wait_ge(d_ctx[which], 16)
                    for c in range(KC):
                        last = turn(bank[:, c * P:(c + 1) * P], ctx_in[:, which * KC + c, :], ident[:, :])
                elif kind == "kx":
                    if which == 0:
                        pe.wait_ge(d_wk2, 16)
                        pe.wait_ge(s_ev["act"], 2)
                    last = mm(bank, wk2[:, :], ctx_t[:, which * BANK:(which + 1) * BANK], start=True, stop=True)
                elif kind == "vx":
                    if which == 0:
                        pe.wait_ge(d_wv2, 16)
                    for c in range(KC):
                        t = (which * KC + c) * P
                        last = mm(bank[:, c * P:(c + 1) * P], ctx_t[:, t:t + P], wv2[:, :], start=True, stop=True)
                elif kind == "x_t":
                    pe.wait_ge(s_xhat, 1)
                    for c in range(NC_):
                        last = turn(bank[:, c * P:(c + 1) * P], x_hat[:, c, :], ident[:, :])
                else:
                    if which == 0:
                        pe.wait_ge(d_wq1 if kind == "q" else d_wk1, 16)
                    if kind == "q" and which == 0:
                        pe.wait_ge(s_ev["dve"], evacuated(index_of("x_t", 0))[1])
                    w = wq1 if kind == "q" else wk1
                    last = mm(bank, w[:, which * P:(which + 1) * P], x_hat_t[:, :], start=True, stop=True)
                last.then_inc(s_item, 1)

            def out_proj1(b, c):
                if b == 0:
                    pe.wait_ge(d_wo1, 16)
                pe.wait_ge(s_o1, NP * (b + 1))
                t = b * S + c * P
                for p in range(NP):
                    last = mm(ps[:, MID_BANK, c * P:(c + 1) * P], o1_t[:, p, t:t + P], wo1[:, p, :],
                              start=p == 0, stop=p == NP - 1)
                if c == C - 1:
                    last.then_inc(s_wo, 1)

            def out_proj2(b):
                if b == 0:
                    pe.wait_ge(d_pad, 32 * HG)
                else:
                    pe.wait_ge(s_lshift, 1)
                pe.wait_ge(s_o2, NG * (b + 1))
                for c in range(C):
                    t = b * S + c * P
                    for hg in range(NG):
                        last = mm(ps[:, MID_BANK, c * P:(c + 1) * P], o2_t[:, hg, t:t + P], wo2[:, hg, :],
                                  start=hg == 0, stop=hg == NG - 1)
                last.then_inc(s_wo, 1)

            def turn_x_hat(k, b):
                pe.wait_ge(s_xhat, k + 1)
                for c in range(C):
                    last = turn(ps[:, MID_BANK, c * P:(c + 1) * P], x_hat[:, b * C + c, :], ident[:, :])
                last.then_inc(s_xhat_ps, 1)

            def query2(b):
                if b == 0:
                    pe.wait_ge(d_wq2, 16)
                pe.wait_ge(s_xhat_t, b + 1)
                mm(ps[:, MID_BANK, S:2 * S], wq2[:, :], x_hat_t[:, b * S:(b + 1) * S],
                   start=True, stop=True).then_inc(s_q2ps, 1)

            def gate(b):
                if b == 0:
                    pe.wait_ge(d_ffn, 16 * 5)
                pe.wait_ge(s_xhat_t, 3 + b)
                for c in range(C):
                    t = b * S + c * P
                    last = mm(ps[:, MID_BANK, S + c * NE:S + (c + 1) * NE], x_hat_t[:, t:t + P], gate_w[:, :],
                              start=True, stop=True)
                last.then_inc(s_logit, 1)

            def between(what):
                kind, b, c = what
                if kind == "wo":
                    out_proj1(b, c)
                elif kind == "turn":
                    turn_x_hat(1 + b, b)
                elif kind == "q":
                    query2(b)
                elif kind == "wo2":
                    out_proj2(b)
                elif kind == "turn2":
                    turn_x_hat(3 + b, b)
                elif kind == "gate":
                    gate(b)

            def scores1(s):
                b, p = divmod(s, NP)
                for r in range(2):
                    if s >= 2:
                        pe.wait_ge(s_exp1, 2 * (s - 2) + r + 1)
                    rows = slice(HD1 * r, HD1 * (r + 1))
                    for c in range(C):
                        last = mm(ps[:, 2 * (s % 2) + r, c * S:(c + 1) * S],
                                  q1_t[rows, p, b * S + c * P:b * S + (c + 1) * P],
                                  k1_t[rows, p, b * S:(b + 1) * S], start=True, stop=True)
                    last.then_inc(s_score1, 1)

            def values1(s):
                b, p = divmod(s, NP)
                pe.wait_ge(s_pt1, 2 * (s + 1))
                if s >= 1:
                    pe.wait_ge(s_o1, s)
                for c in range(C):
                    for r in range(2):
                        h = 2 * p + r
                        last = mm(ps[HD1 * r:HD1 * (r + 1), O_BANK, 0:S],
                                  v1[:, b * C + c, h * HD1:(h + 1) * HD1],
                                  prob1_t[:, s % 2, r, c * S:(c + 1) * S], start=c == 0, stop=c == C - 1)
                last.then_inc(s_pv1, 1)

            def turn1(s):
                for r in range(2):
                    pe.wait_ge(s_norm1, 2 * s + r + 1)
                    if s >= 1:
                        pe.wait_ge(s_pt1, 2 * (s - 1) + r + 1)
                    elif r == 0:
                        pe.wait_ge(s_vev[0], NC_)
                        pe.wait_ge(s_vev[1], NC_)
                    for c in range(C):
                        for i in range(C):
                            last = turn(ps[:, PT_BANK + r, i * S + c * P:i * S + (c + 1) * P],
                                        prob1[:, s % 3, r, c * S + i * P:c * S + (i + 1) * P], ident[:, :])
                    last.then_inc(s_turn1, 1)

            def scores2(n):
                b, h = divmod(n, H2)
                if n == 0:
                    pe.wait_ge(d_kstack, 16 * PARTS * PARTS)
                if h == 0:
                    pe.wait_ge(d_qstack[b], 16 * PARTS)
                for c in range(C):
                    if n >= 2:
                        pe.wait_ge(s_low2, C * (n - 2) + c + 1)
                    else:
                        pe.wait_ge(s_exp1, 2 * (N_SELF - 2 + n) + c + 1)
                    t = b * S + c * P
                    mm(ps[:, 2 * (n % 2) + c, :], q2_stack[:, h, t:t + P],
                       k2_stack[:, h, b * SK:(b + 1) * SK], start=True, stop=True).then_inc(s_score2, 1)

            def values2(k, half):
                b, hg = divmod(k, NG)
                if half == 0:
                    pe.wait_ge(s_pt2a, HG * (k + 1))
                    pe.wait_ge(s_pt2b, HG * (k + 1))
                    if k >= 1:
                        pe.wait_ge(s_orec, k)
                    else:
                        pe.wait_ge(s_o1, N_SELF)
                for kc in (2 * half, 2 * half + 1):
                    for g in range(HG):
                        mm(ps[CW * g:CW * (g + 1), O_BANK, 0:S], v2[:, b * KC + kc, HG * hg + g, :],
                           prob2_t[(HG * k + g) % PT_SLOTS][:, kc, :], start=kc == 0, stop=kc == KC - 1)
                if half == 1:
                    pe.wait_ge(s_wide2, k + 1)
                    for c in range(C):
                        last = turn(ps[:, O_BANK, S + c * P:S + (c + 1) * P], rec2_wide[:, k % 2, c, :], ident[:, :])
                    last.then_inc(s_orec_ps, 1)

            def turn2(n):
                pe.wait_ge(s_exp2, C * (n + 1))
                for half, done, free in ((0, s_turn2a, s_pt2a), (1, s_turn2b, s_pt2b)):
                    if n >= 1:
                        pe.wait_ge(free, n)
                    else:
                        pe.wait_ge(s_pt1, 2 * N_SELF)
                    for k2 in range(2):
                        kc = 2 * half + k2
                        for c in range(C):
                            last = turn(ps[:, PT_BANK + half, k2 * S + c * P:k2 * S + (c + 1) * P],
                                        prob2[n % 3][:, c, kc * P:(kc + 1) * P], ident[:, :])
                    last.then_inc(done, 1)

            def values_of_tokens(g):
                for i, (c, half) in enumerate(V_ITEMS[g]):
                    if g == 0:
                        if i == 0:
                            pe.wait_ge(d_wv1, 16)
                        engine, value = evacuated(max(j for j in range(len(ITEMS)) if j % 8 == V_BANKS[i]))
                        pe.wait_ge(s_ev[engine], value)
                    else:
                        pe.wait_ge(s_vev[half], 2 * (g - 1) + i // 2 + 1)
                    mm(ps[:, V_BANKS[i], :], x_hat_t[:, c * P:(c + 1) * P],
                       wv1[:, half * BANK:(half + 1) * BANK], start=True, stop=True).then_inc(s_v, 1)

            for g in range(LAST_G + 1):
                n = g - N_SELF
                if g == 0:
                    values_of_tokens(0)
                if g < N_SELF:
                    scores1(g)
                if 0 <= n < N_CROSS:
                    scores2(n)
                if g >= 1 and g in V_ITEMS:
                    values_of_tokens(g)
                for what in BETWEEN.get(g, ()):
                    between(what)
                if 0 <= g - LAG_V < N_SELF:
                    values1(g - LAG_V)
                if n >= HG + LAG_V:
                    k, half = divmod(n - LAG_V, HG)
                    if half < 2 and 1 <= k <= B * NG:
                        values2(k - 1, half)
                if 0 <= g - LAG_T < N_SELF:
                    turn1(g - LAG_T)
                if 0 <= n - LAG_T < N_CROSS:
                    turn2(n - LAG_T)

            pe.wait_ge(s_low2, C * N_CROSS)
            pe.wait_ge(s_pt2a, N_CROSS)
            pe.wait_ge(s_pt2b, N_CROSS)
            for i in range(N_FFN + 1):
                if i < N_FFN:
                    b, k = divmod(i, NE + 1)
                    e, rows = (k - 1) % (NE + 1), slice(b * S, (b + 1) * S)
                    if i >= 2:
                        pe.wait_ge(s_silu, i - 1)
                    for f in range(FC):
                        last = mm(ps[:, i % 2, f * S:(f + 1) * S], wg[:, e, f * P:(f + 1) * P], x_hat_t[:, rows],
                                  start=True, stop=True)
                    last.then_inc(s_g, 1)
                    if i >= 2:
                        pe.wait_ge(s_hid, i - 1)
                    for f in range(FC):
                        last = mm(ps[:, 2 + i % 2, f * S:(f + 1) * S], wu[:, e, f * P:(f + 1) * P], x_hat_t[:, rows],
                                  start=True, stop=True)
                    last.then_inc(s_u, 1)
                if i >= 1:
                    e = ((i - 1) % (NE + 1) - 1) % (NE + 1)
                    if i == 1:
                        pe.wait_ge(d_wd, 32)
                    pe.wait_ge(s_hid, i)
                    if i >= 3:
                        pe.wait_ge(s_ypart, i - 2)
                    for c in range(C):
                        for f in range(FC):
                            last = mm(ps[:, 4 + (i - 1) % 2, c * P:(c + 1) * P],
                                      hid[(i - 1) % 2][:, f, c * P:(c + 1) * P], wd[:, e, f, :],
                                      start=f == 0, stop=f == FC - 1)
                    last.then_inc(s_y, 1)
                for what in FFN_BETWEEN.get(i, ()):
                    between(what)

        @block.vector
        def _(dve):
            chain = [0]

            def link(ins):
                chain[0] += 1
                ins.then_inc(s_dve, 1)
                dve.wait_ge(s_dve, chain[0])

            def statistics(k, src, first, count):
                for c in range(first, first + count):
                    ins = nc.vector.bn_stats(stats[:, c, :], src[:, c, :])
                link(ins)
                for c in range(first, first + count):
                    ins = nc.vector.bn_aggr(mean_var[:, c, :], stats[:, c, :])
                ins.then_inc(s_var, 1)

            def normalise(k, src, first, count):
                dve.wait_ge(s_var, k + 1)
                dve.wait_ge(s_rstd, k + 1)
                for c in range(first, first + count):
                    ins = nc.vector.tensor_scalar(x_hat[:, c, :], src[:, c, :], mean_var[:, c, 0:1],
                                                  rstd[:, c:c + 1], ALU.subtract, ALU.mult)
                ins.then_inc(s_xhat, 1)

            dve.wait_ge(d_x, 16)
            statistics(0, x_in, 0, NC_)
            normalise(0, x_in, 0, NC_)

            def split(full, rest_, parts):
                link(nc.vector.tensor_copy(parts[:, 0, :], full))
                link(nc.vector.tensor_tensor(rest_, full, parts[:, 0, :], ALU.subtract))
                link(nc.vector.tensor_copy(parts[:, 1, :], rest_))
                return nc.vector.tensor_tensor(parts[:, 2, :], rest_, parts[:, 1, :], ALU.subtract)

            for j, (kind, which, engine) in enumerate(ITEMS):
                if engine != "dve":
                    continue
                if (kind, which) == ("k", 0):
                    dve.wait_ge(d_bias, 16)
                dve.wait_ge(s_item, j + 1)
                bank = ps[:, j % 8, :]
                if kind == "x_t":
                    ins = nc.vector.tensor_copy(x_hat_t[:, :], bank)
                else:
                    ins = nc.vector.tensor_scalar(k1_t[:, which, :], bank, bias1[:, 1, which:which + 1], None, ALU.add)
                ins.then_inc(s_ev["dve"], 1)
                if (kind, which) == ("k", 1):
                    dve.wait_ge(s_ev["act"], evacuated(index_of("kx", 1))[1])
                    split(k2_t, k2_rest, k2_parts).then_inc(s_kparts, 1)
                if (kind, which) == ("k", 4):
                    dve.wait_ge(d_mask, 16)
                    nc.vector.tensor_scalar(mask_add[:, :, :], mask_in, 0, MASKED, ALU.is_equal, ALU.mult
                                            ).then_inc(s_maskadd, 1)

            def residual(k, b, dst, src, done):
                dve.wait_ge(s_wo, k + 1)
                ins = nc.vector.tensor_tensor(dst[:, b * C:(b + 1) * C, :],
                                              ps[:, MID_BANK, 0:C * P].rearrange("p (c n) -> p c n", c=C),
                                              src[:, b * C:(b + 1) * C, :], ALU.add)
                ins.then_inc(done, 1)
                dve.wait_ge(done, b + 1)

            def between(what):
                kind, b, c = what
                if kind == "residual":
                    dve.wait_ge(s_xbo, C * (b + 1))
                    residual(b, b, x1, x_bo, s_x1)
                    statistics(1 + b, x1, b * C, C)
                elif kind == "x_hat":
                    normalise(1 + b, x1, b * C, C)
                elif kind == "parts":
                    dve.wait_ge(s_q2ps, b + 1)
                    if b >= 1:
                        dve.wait_ge(d_qdram[b - 1], 16)
                    link(nc.vector.tensor_scalar(q2_t[:, :], ps[:, MID_BANK, S:2 * S], bias2[:, 0:1], -SCALE2,
                                                 ALU.add, ALU.mult))
                    split(q2_t[:, :], q2_rest[:, :], q2_parts).then_inc(s_qparts, 1)
                elif kind == "residual2":
                    dve.wait_ge(s_x1bo, C * (b + 1))
                    residual(2 + b, b, x2, x1_bo, s_x2)
                    statistics(3 + b, x2, b * C, C)
                elif kind == "x_hat2":
                    normalise(3 + b, x2, b * C, C)
                elif kind == "shift":
                    shift_logits(b)
                elif kind == "weights":
                    gate_weights(b)

            v = nc.vector

            def rows_of(b):
                return slice(b * C, (b + 1) * C)

            def wide(i, b):
                return col[:, i, rows_of(b)].unsqueeze(2).to_broadcast([P, C, NE])

            def shift_logits(b):
                cs = rows_of(b)
                dve.wait_ge(s_logit, b + 1)
                link(v.tensor_copy(logit[:, cs, :],
                                   ps[:, MID_BANK, S:S + C * NE].rearrange("p (c e) -> p c e", c=C)))
                link(v.tensor_reduce(col[:, 0, cs], logit[:, cs, :], AX.X, ALU.max))
                v.tensor_tensor(logit[:, cs, :], logit[:, cs, :], wide(0, b), ALU.subtract).then_inc(s_lshift, 1)

            def gate_weights(b):
                cs = rows_of(b)
                dve.wait_ge(s_gexp, b + 1)
                link(v.tensor_reduce(col[:, 1, cs], gate_e[:, cs, :], AX.X, ALU.add))
                link(v.reciprocal(col[:, 2, cs], col[:, 1, cs]))
                link(v.tensor_tensor(gate_s[:, cs, :], gate_e[:, cs, :], wide(2, b), ALU.mult))

                def first_largest(values, to):
                    link(v.tensor_reduce(col[:, 3, cs], values, AX.X, ALU.max))
                    link(v.tensor_tensor(pick[:, cs, :], values, wide(3, b), ALU.is_equal))
                    link(v.tensor_tensor(pick[:, cs, :], pick[:, cs, :], rank[:, cs, :], ALU.mult))
                    link(v.tensor_reduce(col[:, 4, cs], pick[:, cs, :], AX.X, ALU.max))
                    link(v.tensor_tensor(to, pick[:, cs, :], wide(4, b), ALU.is_equal))

                first_largest(gate_s[:, cs, :], pick1[:, cs, :])
                link(v.scalar_tensor_tensor(out=rest[:, cs, :], in0=pick1[:, cs, :], scalar=-2.0,
                                            in1=gate_s[:, cs, :], op0=ALU.mult, op1=ALU.add))
                first_largest(rest[:, cs, :], pick2[:, cs, :])
                link(v.tensor_tensor(pick[:, cs, :], pick1[:, cs, :], pick2[:, cs, :], ALU.add))
                link(v.tensor_tensor(pick[:, cs, :], pick[:, cs, :], gate_s[:, cs, :], ALU.mult))
                link(v.tensor_reduce(col[:, 5, cs], pick[:, cs, :], AX.X, ALU.add))
                link(v.tensor_scalar(col[:, 5, cs], col[:, 5, cs], 1e-20, None, ALU.add))
                link(v.reciprocal(col[:, 0, cs], col[:, 5, cs]))
                link(v.tensor_tensor(w_e[:, cs, :], pick[:, cs, :], wide(0, b), ALU.mult))

            def low_scores1(s):
                for r in range(2):
                    dve.wait_ge(s_score1, 2 * s + r + 1)
                    nc.vector.tensor_reduce(low1[:, s % 2, r, :],
                                            ps[:, 2 * (s % 2) + r, :].rearrange("p (c i) -> p c i", c=C),
                                            AX.X, ALU.min).then_inc(s_low1, 1)

            def low_scores2(n):
                for c in range(C):
                    dve.wait_ge(s_score2, C * n + c + 1)
                    if n >= 2:
                        dve.wait_ge(s_exp2, C * (n - 2) + c + 1)
                    nc.vector.tensor_tensor_reduce(out=score2[n % 2][:, c, :], in0=ps[:, 2 * (n % 2) + c, :],
                                                   in1=mask_add[:, c, :], scale=1.0, scalar=3e38,
                                                   op0=ALU.add, op1=ALU.min, accum_out=low2[:, n % 2, c:c + 1]
                                                   ).then_inc(s_low2, 1)

            dve.wait_ge(s_maskadd, 1)
            dve.wait_ge(s_const, 1 + NE)
            for g in range(LAST_G + 1):
                n = g - N_SELF
                if 1 <= g <= N_SELF:
                    for r in range(2):
                        dve.wait_ge(s_exp1, 2 * (g - 1) + r + 1)
                        nc.vector.reciprocal(rec1[:, (g - 1) % 2, r, :], sum1[:, (g - 1) % 2, r, :]
                                             ).then_inc(s_rec1, 1)
                for i, (c, half) in enumerate(V_ITEMS.get(g, ())):
                    if half == 1:
                        dve.wait_ge(s_v, len(V_BANKS) * g + i + 1)
                        nc.vector.tensor_copy(v1[:, c, BANK:2 * BANK], ps[:, V_BANKS[i], :]).then_inc(s_vev[1], 1)
                if g < N_SELF:
                    low_scores1(g)
                if 0 <= n < N_CROSS:
                    low_scores2(n)
                for what in BETWEEN.get(g, ()):
                    between(what)
                if n >= HG and n % HG == 0 and n <= N_CROSS:
                    k = n // HG - 1
                    dve.wait_ge(s_exp2, C * n)
                    nc.vector.reciprocal(rec2[:, k % 2, :, :], sum2[:, k % 2, :, :]).then_inc(s_rec2, 1)
                if 0 <= g - LAG_T < N_SELF:
                    for r in range(2):
                        dve.wait_ge(s_turn1, 2 * (g - LAG_T) + r + 1)
                        nc.vector.tensor_copy(prob1_t[:, g % 2, r, :], ps[:, PT_BANK + r, :]).then_inc(s_pt1, 1)
                if 0 <= n - LAG_T < N_CROSS:
                    dve.wait_ge(s_turn2a, n - LAG_T + 1)
                    nc.vector.tensor_copy(prob2_t[(n - LAG_T) % PT_SLOTS][:, 0:2, :],
                                          ps[:, PT_BANK, :].rearrange("p (k t) -> p k t", k=2)).then_inc(s_pt2a, 1)

            def bank_y(i):
                return ps[:, 4 + i % 2, 0:C * D].rearrange("p (c n) -> p c n", c=C)

            def outputs(i):
                b, k = divmod(i, NE + 1)
                cs = rows_of(b)
                dve.wait_ge(s_y, i + 1)
                if k == 0:
                    v.tensor_tensor(acc[:, cs, :], bank_y(i), x2[:, cs, :], ALU.add).then_inc(s_ypart, 1)
                elif k < NE:
                    if k >= 3:
                        dve.wait_ge(s_acc, b * (NE - 1) + k - 2)
                    v.tensor_tensor(y_part[k % 2], bank_y(i), w_e[:, cs, k - 1:k].to_broadcast([P, C, D]),
                                    ALU.mult).then_inc(s_ypart, 1)
                else:
                    dve.wait_ge(s_acc, (b + 1) * (NE - 1))
                    for c in range(C):
                        ins = v.scalar_tensor_tensor(out=y_out[:, b * C + c, :], in0=bank_y(i)[:, c, :],
                                                     scalar=w_e[:, b * C + c, k - 1:k], in1=acc[:, b * C + c, :],
                                                     op0=ALU.mult, op1=ALU.add)
                    ins.then_inc(s_ypart, 1)

            for i in range(N_FFN + 1):
                if i < N_FFN:
                    dve.wait_ge(s_silu, i + 1)
                    dve.wait_ge(s_u, i + 1)
                    if i >= 2:
                        dve.wait_ge(s_y, i - 1)
                    v.tensor_tensor(hid[i % 2], silu[i % 2].rearrange("p (f t) -> p f t", f=FC),
                                    ps[:, 2 + i % 2, :].rearrange("p (f t) -> p f t", f=FC), ALU.mult
                                    ).then_inc(s_hid, 1)
                if i >= 1:
                    outputs(i - 1)
                for what in FFN_BETWEEN.get(i, ()):
                    between(what)


INPUTS = ["x", "ctx_1024", "mask_1x1xSxS2_ik1", "biases"]
INPUTS += ["L0_attn_" + w for w in ("Wq", "Wk", "Wv", "Wo", "bo")]
INPUTS += ["L0_xattn_" + w for w in ("Wq", "Wk", "Wv", "Wo", "bv", "bo")]
INPUTS += ["L0_ffn_" + w for w in ("gate_w", "w_gate", "w_up", "w_down", "ws_gate", "ws_up", "ws_down")]


def kernel(**inputs):
    import numpy as np
    import concourse.bacc as bacc
    from concourse.bass_utils import run_bass_kernel_spmd

    nc = bacc.Bacc("TRN2", target_bir_lowering=False, num_devices=1)
    laid = dict(inputs)
    columns = [np.asarray(inputs["L0_attn_" + w]).reshape(NP, P).T for w in ("bq", "bk", "bv")]
    columns += [np.asarray(inputs["L0_xattn_" + w]).reshape(H2, HD2).T.reshape(P, 1) for w in ("bq", "bk")]
    for w in ("L0_xattn_Wq", "L0_xattn_Wk"):
        laid[w] = np.asarray(inputs[w]).reshape(D, H2, HD2).transpose(0, 2, 1).reshape(D, D)
    laid["biases"] = np.concatenate(columns, axis=1)
    laid["L0_xattn_bv"] = np.asarray(inputs["L0_xattn_bv"]).reshape(NG, HG, HD2).transpose(1, 2, 0)
    arrays, aps = {}, {}
    for name in INPUTS:
        array = np.ascontiguousarray(laid[name])
        arrays[f"in_{name}"] = array
        aps[name] = nc.dram_tensor(f"in_{name}", array.shape, mybir.dt.from_np(array.dtype), kind="ExternalInput").ap()
    out = nc.dram_tensor("out", (B, S, D), F32, kind="ExternalOutput").ap()
    build(nc, aps, out)
    return run_bass_kernel_spmd(nc, [arrays], core_ids=[0]).results[0]["out"]
```

```python
from contextlib import ExitStack

import concourse.bass as bass
from concourse import mybir

F32 = mybir.dt.float32
BF16 = mybir.dt.bfloat16
F32R = mybir.dt.float32r
ALU = mybir.AluOpType
ACT = mybir.ActivationFunctionType
AX = mybir.AxisListType

P = 128
B, S, D = 2, 256, 128
C = S // P
NC_ = B * C
T = B * S
H1, HD1 = 16, 64
NP = H1 // 2
H2, HD2 = 16, 8
SK = 512
KC = SK // P
TK = B * SK
PARTS = 3
KSTACK = PARTS * PARTS * HD2
HG = 4
NG = H2 // HG
CW = P // HG
NE, FF = 8, 256
FC = FF // P
EPS = 1e-5
BIG_PARTS = ((0, 0), (0, 1), (1, 0))
MASKED = 1e30
BANK = 512
SCALE1 = 1.0 / 8.0
SCALE2 = float(HD2) ** -0.5
PT_SLOTS = 8
WARM_UP = 8

PT_BANK, O_BANK, MID_BANK = 4, 6, 7

N_SELF = B * NP
N_CROSS = B * H2
LAG_T, LAG_V = 2, 3
LAST_G = N_SELF + N_CROSS + LAG_T + 1
BETWEEN = {
    11: [("residual", 0), ("x_hat", 0)],
    12: [("turn", 0), ("turned", 0)],
    13: [("q", 0), ("parts", 0)],
    N_SELF + 3: [("residual", 1)],
    N_SELF + 4: [("x_hat", 1)],
    N_SELF + 5: [("turn", 1)],
    N_SELF + 6: [("turned", 1)],
    N_SELF + 7: [("q", 1)],
    N_SELF + 8: [("parts", 1)],
    N_SELF + 23: [("turn_o2", 0)],
    N_SELF + 24: [("turned_o2", 0)],
    N_SELF + 25: [("wo2", 0)],
    N_SELF + 26: [("residual2", 0)],
    N_SELF + 27: [("x_hat2", 0)],
    N_SELF + 28: [("turn2", 0)],
    N_SELF + 29: [("turned2", 0)],
    N_SELF + 30: [("gate", 0)],
    N_SELF + 31: [("shift", 0)],
    N_SELF + 32: [("gate_exp", 0)],
}
VALUES2 = {}
for k in range(B * NG):
    later = {B * NG - 2: (1, 1, 2, 2), B * NG - 1: (0, 0, 0, 0)}.get(k, (1, 1, 2, 3))
    for kc in range(KC):
        VALUES2.setdefault(HG * (k + 1) + LAG_T + later[kc], []).append((k, kc))
O2_BANK = [O_BANK] * (B * NG - 1) + [MID_BANK]
O_READY = {max(n for n in VALUES2 if (k, KC - 1) in VALUES2[n]) + 1: k for k in range(B * NG)}
SPLIT_N = 5
FFN_G, FFN_EARLY = N_SELF + N_CROSS + 1, 3
LAG_D = 2
N_FFN = B * (NE + 1)
FFN_BETWEEN = {
    1: [("weights", 0)],
    3: [("turn_o2", 1), ("turned_o2", 1)],
    4: [("wo2", 1), ("residual2", 1)],
    5: [("x_hat2", 1)],
    6: [("turn2", 1), ("turned2", 1)],
    7: [("gate", 1)],
    8: [("shift", 1), ("gate_exp", 1)],
    11: [("weights", 1)],
}


WO1 = {p + LAG_V + 1: [(0, p)] for p in range(NP)}
for p in range(NP):
    WO1.setdefault(max(NP + p + LAG_V + 1, 14 + p // 2), []).append((1, p))


def items():
    out = [("ctx_t", 0, "act"), ("ctx_t", 1, "act"), ("kx", 0, "act"), ("x_t", 0, "dve"), ("kx", 1, "act")]
    for p in range(NP):
        if p == 2:
            out += [("vx", 0, "act"), ("vx", 1, "act")]
        out += [("q", p, "act"), ("k", p, "dve")]
    return out


ITEMS = items()
V_BANKS = (7, 4, 5, 6)
V_ITEMS = {g: [(c, half) for c in (2 * g, 2 * g + 1) for half in (0, 1)] for g in range(NC_ // 2)}


def evacuated(j):
    engine = ITEMS[j][2]
    return engine, sum(1 for x in ITEMS[:j + 1] if x[2] == engine)


def index_of(kind, which):
    return [x[:2] for x in ITEMS].index((kind, which))


def build(nc, a, out):
    with ExitStack() as ctx:
        def sb(name, shape, dt=F32):
            return ctx.enter_context(nc.sbuf_tensor(name, shape, dt))

        def retired(name, shape, dt=F32):
            with nc.sbuf_tensor(name, shape, dt) as t:
                return t

        def part_tiles(name, count):
            return [sb(f"{name}_parts{i}", [P, FF], F32R) for i in range(count)]

        def sem(name):
            return ctx.enter_context(nc.semaphore(name))

        ps = ctx.enter_context(nc.psum_tensor("ps", [P, 8, BANK], F32))

        ident = sb("ident", [P, P])
        x_in = sb("x_in", [P, NC_, D])
        x_bo = sb("x_bo", [P, NC_, D])
        x1 = sb("x1", [P, NC_, D])
        x1_bo = x_bo
        x2 = x_in
        bo1 = sb("bo1", [P, D])
        bo2 = sb("bo2", [P, D])
        stats = sb("stats", [P, NC_, 6])
        mean_var = sb("mean_var", [P, NC_, 2])
        var_eps = sb("var_eps", [P, NC_])
        minus_half = sb("minus_half", [P, NC_])
        rstd = sb("rstd", [P, NC_])
        x_hat = sb("x_hat", [P, NC_, D])
        x_hat_t = sb("x_hat_t", [P, T])
        w_in1 = retired("w_in1", [P, 3, H1 * HD1])
        wg = retired("wg", [P, NE + 1, FF])
        tiles = part_tiles("w_in1", 12)
        late_tiles, tiles = tiles[:NE], tiles[NE + 1:]
        wq1, wk1, wv1 = (w_in1[:, i, :] for i in range(3))
        wo1 = sb("wo1", [P, NP, D])
        biases = sb("biases", [P, 3 * NP + 2])
        bias1 = biases[:, 0:3 * NP].rearrange("p (i n) -> p i n", i=3)
        bias2 = biases[:, 3 * NP:3 * NP + 2]
        bq1_s = sb("bq1_s", [P, NP])
        q1_t = sb("q1_t", [P, NP, T])
        k1_t = retired("k1_t", [P, NP, T])
        place_k1 = sb("place_k1", [P, NP // 2, T])
        tiles += part_tiles("k1", 8)
        v1 = retired("v1", [P, NC_, H1 * HD1])
        wd = sb("wd", [P, NE + 1, FC, D])
        tiles += part_tiles("v1", 7)
        v_parts = retired("v_parts", [P, 2, H1 * HD1 + T], F32R)
        wv1_parts, xv_parts = v_parts[:, :, 0:H1 * HD1], v_parts[:, :, H1 * HD1:]
        o1_t = retired("o1_t", [P, B, NP, S])
        place_o1 = sb("place_o1", [P, NP, S])
        tiles += part_tiles("o1", 8)
        low1 = sb("low1", [P, 2, 2, C])
        sum1 = sb("sum1", [P, 2, 2, C])
        rec1 = sb("rec1", [P, 2, 2, C])
        prob1 = sb("prob1", [P, 3, 2, C * S])
        prob1_t = sb("prob1_t", [P, 2, 2, C * S])
        prob1_flat = prob1[:, :, :, :].rearrange("p a r n -> p (a r n)")
        prob1_t_flat = prob1_t[:, :, :, :].rearrange("p a r n -> p (a r n)")

        k2_parts = prob1_flat[:, 0:PARTS * TK // 2].bitcast(BF16).rearrange("p (j t) -> p j t", j=PARTS)
        mask_in = prob1_t_flat[:, 0:C * SK].bitcast(mybir.dt.int32).rearrange("p (c k) -> p c k", c=C)
        ctx_in = prob1_t_flat[:, C * SK:C * SK + B * KC * D].rearrange("p (c d) -> p c d", d=D)
        context = retired("context", [P, 3, TK])
        wu = sb("wu", [P, NE + 1, FF])
        tiles += part_tiles("context", 3)
        ctx_t, k2_t, k2_rest = (context[:, i, :] for i in range(3))
        wq2 = sb("wq2", [P, D])
        wk2 = sb("wk2", [P, D])
        wv2 = sb("wv2", [P, D])
        wo2 = sb("wo2", [P, D])
        bv2 = sb("bv2", [P, H2, HD2])
        mask_add = sb("mask_add", [P, C, SK])
        q2_t = sb("q2_t", [P, S])
        q2_rest = sb("q2_rest", [P, S])
        q2_parts = sb("q2_parts", [P, PARTS, S], BF16)
        k2_stack = sb("k2_stack", [KSTACK, H2, TK], BF16)
        q2_stack = sb("q2_stack", [KSTACK, H2, T], BF16)
        v2 = sb("v2", [P, B * KC, H2, CW])
        low2 = sb("low2", [P, 2, C])
        o_raw = sb("o_raw", [P, S])
        rec2 = sb("rec2", [P, C, HG])
        o2 = sb("o2", [P, NC_, D])
        o2_t = sb("o2_t", [P, S])

        def attn_tile(t, i):
            return t[:, 2 * i:2 * i + 2, :].rearrange("p a n -> p (a n)")

        score2 = [attn_tile(q1_t, i).rearrange("p (c k) -> p c k", c=C) for i in (0, 1)]
        prob2 = [attn_tile(*x).rearrange("p (c k) -> p c k", c=C) for x in ((q1_t, 2), (q1_t, 3), (place_k1, 0))]
        prob2_t = [attn_tile(place_k1, 1)]
        prob2_t += [prob1_flat[:, i * KC * S:(i + 1) * KC * S] for i in range(3)]
        prob2_t += [prob1_t_flat[:, i * KC * S:(i + 1) * KC * S] for i in range(2)]
        prob2_t = [x.rearrange("p (k t) -> p k t", t=S) for x in prob2_t]
        prob2_t += [place_o1[:, KC * i:KC * (i + 1), :] for i in range(2)]

        silu = [q1_t[:, i, :] for i in (0, 1)]
        hid = [q1_t[:, i, :].rearrange("p (f t) -> p f t", f=FC) for i in (2, 3, 4)]
        y_part = [place_k1[:, 2 + i, 0:C * D].rearrange("p (c n) -> p c n", c=C) for i in (0, 1)]
        acc = place_k1[:, 0, :].rearrange("p (c n) -> p c n", c=NC_)
        y_out = place_k1[:, 1, :].rearrange("p (c n) -> p c n", c=NC_)
        tiles += part_tiles("own", 2 * (B + 2 * (NE + 1)) - len(tiles) - len(late_tiles))
        tiles += late_tiles
        pairs = [tiles[i:i + 2] for i in range(0, len(tiles), 2)]
        x_parts, w_parts = pairs[:B], (pairs[B:B + NE + 1], pairs[B + NE + 1:])

        gate_w = sb("gate_w", [P, NE])
        rank = sb("rank", [P, NC_, NE])
        logit = sb("logit", [P, NC_, NE])
        gate_e = sb("gate_e", [P, NC_, NE])
        gate_s = sb("gate_s", [P, NC_, NE])
        pick = sb("pick", [P, NC_, NE])
        pick1 = sb("pick1", [P, NC_, NE])
        pick2 = sb("pick2", [P, NC_, NE])
        rest = sb("rest", [P, NC_, NE])
        w_e = sb("w_e", [P, NC_, NE])
        col = sb("col", [P, 6, NC_])

        k2_dram = nc.dram_tensor("k2_dram", [PARTS, D, TK], BF16, kind="Internal").ap()
        q2_dram = nc.dram_tensor("q2_dram", [B, PARTS, D, S], BF16, kind="Internal").ap()

        d_x, d_wk2, d_wv2, d_wq2 = map(sem, ("d_x", "d_wk2", "d_wv2", "d_wq2"))
        d_ctx = [sem(f"d_ctx{b}") for b in range(B)]
        d_wq1, d_wk1, d_wv1, d_wo1 = map(sem, ("d_wq1", "d_wk1", "d_wv1", "d_wo1"))
        d_bias, d_mask, d_bo, d_wo2, d_ffn, d_wd = map(sem, ("d_bias", "d_mask", "d_bo", "d_wo2", "d_ffn", "d_wd"))
        d_kdram, d_kstack, d_out = map(sem, ("d_kdram", "d_kstack", "d_out"))
        d_qdram = [sem(f"d_qdram{b}") for b in range(B)]
        d_qstack = [sem(f"d_qstack{b}") for b in range(B)]
        s_const, s_ident = map(sem, ("s_const", "s_ident"))
        s_dve, s_pool = map(sem, ("s_dve", "s_pool"))
        s_v = sem("s_v")
        s_vev = {0: sem("s_vev_act"), 1: sem("s_vev_dve")}
        s_item = sem("s_item")
        s_ev = {"act": sem("s_ev_act"), "dve": sem("s_ev_dve")}
        s_bq = sem("s_bq")
        s_var, s_rstd, s_xhat, s_xhat_ps, s_xhat_t = map(sem, ("s_var", "s_rstd", "s_xhat", "s_xhat_ps", "s_xhat_t"))
        s_kparts, s_qparts, s_maskadd = map(sem, ("s_kparts", "s_qparts", "s_maskadd"))
        s_xbo, s_x1, s_x1bo, s_x2 = map(sem, ("s_xbo", "s_x1", "s_x1bo", "s_x2"))
        s_score1, s_low1, s_exp1, s_rec1, s_norm1 = map(sem, ("s_score1", "s_low1", "s_exp1", "s_rec1", "s_norm1"))
        s_turn1, s_pt1, s_pv1, s_o1 = map(sem, ("s_turn1", "s_pt1", "s_pv1", "s_o1"))
        s_wo, s_q2ps = map(sem, ("s_wo", "s_q2ps"))
        s_v2 = sem("s_v2")
        s_score2, s_low2, s_exp2 = map(sem, ("s_score2", "s_low2", "s_exp2"))
        s_turn2a, s_turn2b, s_pt2a, s_pt2b = map(sem, ("s_turn2a", "s_turn2b", "s_pt2a", "s_pt2b"))
        s_pv2, s_oraw, s_oturn, s_o2 = map(sem, ("s_pv2", "s_oraw", "s_oturn", "s_o2"))
        s_o2turn, s_o2t = map(sem, ("s_o2turn", "s_o2t"))
        s_vparts, s_wparts, s_xparts = map(sem, ("s_vparts", "s_wparts", "s_xparts"))
        s_logit, s_lshift, s_gexp, s_we = map(sem, ("s_logit", "s_lshift", "s_gexp", "s_we"))
        s_g, s_u, s_silu, s_hid, s_y, s_ypart, s_acc = map(sem, (
            "s_g", "s_u", "s_silu", "s_hid", "s_y", "s_ypart", "s_acc"))

        def chunks(ap):
            return ap.rearrange("b (c p) d -> p (b c) d", p=P)

        block = ctx.enter_context(nc.Block())

        @block.sync
        def _(sp):
            def load(dst, src, s):
                sp.dma_start(dst, src).then_inc(s, 16)

            load(x_in[:, :, :], chunks(a["x"]), d_x)
            for b in range(B):
                load(ctx_in[:, b * KC:(b + 1) * KC, :], chunks(a["ctx_1024"])[:, b * KC:(b + 1) * KC, :], d_ctx[b])
            load(wk2[:, :], a["L0_xattn_Wk"], d_wk2)
            load(wq1, a["L0_attn_Wq"], d_wq1)
            load(wk1, a["L0_attn_Wk"], d_wk1)
            load(wv2[:, :], a["L0_xattn_Wv"], d_wv2)
            load(wv1, a["L0_attn_Wv"], d_wv1)
            load(mask_in, a["mask_1x1xSxS2_ik1"].rearrange("a b (c p) k -> p (a b c) k", p=P), d_mask)
            load(wq2[:, :], a["L0_xattn_Wq"], d_wq2)
            load(wo1[:, :, :], a["L0_attn_Wo"].rearrange("(p r) n -> r p n", r=P), d_wo1)
            load(wo2[:, :], a["L0_xattn_Wo"], d_wo2)
            sp.wait_ge(s_kparts, 1)
            load(k2_dram.rearrange("j r t -> r j t"), k2_parts, d_kdram)
            sp.wait_ge(d_kdram, 16)
            for j in range(PARTS):
                for i in range(PARTS):
                    r = (j * PARTS + i) * HD2
                    load(k2_stack[r:r + HD2, :, :], k2_dram[j].rearrange("(d h) t -> d h t", d=HD2), d_kstack)
            sp.wait_ge(s_v, NC_ * 2)
            load(wg[:, 0:NE, :], a["L0_ffn_w_gate"].rearrange("e d f -> d e f"), d_ffn)
            load(wu[:, 0:NE, :], a["L0_ffn_w_up"].rearrange("e d f -> d e f"), d_ffn)
            load(wg[:, NE, :], a["L0_ffn_ws_gate"], d_ffn)
            load(wu[:, NE, :], a["L0_ffn_ws_up"], d_ffn)
            load(gate_w[:, :], a["L0_ffn_gate_w"], d_ffn)
            for b in range(B):
                sp.wait_ge(s_qparts, b + 1)
                load(q2_dram[b].rearrange("i r t -> r i t"), q2_parts[:, :, :], d_qdram[b])
                sp.wait_ge(d_qdram[b], 16)
                for j in range(PARTS):
                    r = j * PARTS * HD2
                    load(q2_stack[r:r + PARTS * HD2, :, b * S:(b + 1) * S],
                         q2_dram[b].rearrange("i (d h) t -> (i d) h t", d=HD2), d_qstack[b])
                if b == 0:
                    sp.wait_ge(s_pv1, N_SELF)
                    load(wd[:, 0:NE, :, :], a["L0_ffn_w_down"].rearrange("e (f r) n -> r e f n", r=P), d_wd)
                    load(wd[:, NE, :, :], a["L0_ffn_ws_down"].rearrange("(f r) n -> r f n", r=P), d_wd)
            out_c = chunks(out)
            for b in range(B):
                sp.wait_ge(s_ypart, (b + 1) * (NE + 1))
                load(out_c[:, b * C:(b + 1) * C, :], y_out[:, b * C:(b + 1) * C, :], d_out)
            sp.wait_ge(d_out, 16 * B)

        @block.gpsimd
        def _(pool):
            chain = [0]

            def link(ins):
                chain[0] += 1
                ins.then_inc(s_pool, 1)
                pool.wait_ge(s_pool, chain[0])

            link(nc.gpsimd.memset(ident[:, :], 0.0))
            nc.gpsimd.affine_select(out=ident[:, :], in_=ident[:, :], compare_op=ALU.not_equal, fill=1.0,
                                    base=0, pattern=[[-1, P]], channel_multiplier=1).then_inc(s_ident, 1)
            link(nc.gpsimd.memset(minus_half[:, :], -0.5))

            def reciprocal_std(k, first, count):
                pool.wait_ge(s_var, k + 1)
                link(nc.gpsimd.tensor_scalar(var_eps[:, first:first + count], mean_var[:, first:first + count, 1],
                                             EPS, None, ALU.add))
                nc.gpsimd.tensor_tensor(rstd[:, first:first + count], var_eps[:, first:first + count],
                                        minus_half[:, first:first + count], ALU.pow).then_inc(s_rstd, 1)

            reciprocal_std(0, 0, NC_)
            nc.gpsimd.memset(v2[:, :, :, HD2 + 1:CW], 0.0)
            nc.gpsimd.memset(v2[:, :, :, HD2:HD2 + 1], 1.0).then_inc(s_const, 1)
            for e in range(NE):
                nc.gpsimd.memset(rank[:, :, e], float(NE - e)).then_inc(s_const, 1)
            pool.dma_start(bo1[:, :], a["L0_attn_bo"].rearrange("(o n) -> o n", o=1).to_broadcast([P, D])).then_inc(d_bo, 16)
            pool.dma_start(bo2[:, :], a["L0_xattn_bo"].rearrange("(o n) -> o n", o=1).to_broadcast([P, D])).then_inc(d_bo, 16)
            pool.dma_start(bv2[:, :, :], a["L0_xattn_bv"].rearrange("(o h d) -> o h d", o=1, d=HD2)
                           .to_broadcast([P, H2, HD2])).then_inc(d_bo, 16)

            def split(full, parts):
                link(nc.gpsimd.tensor_copy(parts[0], full))
                return nc.gpsimd.tensor_tensor(parts[1], full, parts[0].bitcast(F32), ALU.subtract)

            pool.wait_ge(d_wv1, 16)
            split(wv1, [wv1_parts[:, i, :] for i in range(2)]).then_inc(s_vparts, 1)
            pool.wait_ge(s_ev["dve"], evacuated(index_of("x_t", 0))[1])
            split(x_hat_t[:, :], [xv_parts[:, i, :] for i in range(2)]).then_inc(s_vparts, 1)
            pool.wait_ge(d_x, 16)
            pool.wait_ge(d_bo, 48)
            for c in range(NC_):
                nc.gpsimd.tensor_tensor(x_bo[:, c, :], x_in[:, c, :], bo1[:, :], ALU.add).then_inc(s_xbo, 1)

            def split_tokens(b):
                pool.wait_ge(s_xhat_t, 3 + b)
                split(x_hat_t[:, b * S:(b + 1) * S], [t[:, :] for t in x_parts[b]]).then_inc(s_xparts, 1)

            def split_weights(i):
                which, k = divmod(i, NE + 1)
                e = (k - 1) % (NE + 1)
                if i == 0:
                    pool.wait_ge(d_ffn, 16 * 5)
                    pool.wait_ge(s_score1, 2 * N_SELF)
                    pool.wait_ge(s_pv1, N_SELF)
                    pool.wait_ge(s_wo, B)
                split((wg, wu)[which][:, e, :], [t[:, :] for t in w_parts[which][e]]).then_inc(s_wparts, 1)

            pool.wait_ge(s_ev["act"], evacuated(index_of("vx", 1))[1])
            for c in range(B * KC):
                nc.gpsimd.tensor_tensor(v2[:, c, :, 0:HD2], v2[:, c, :, 0:HD2], bv2[:, :, :], ALU.add
                                        ).then_inc(s_v2, 1)

            def add_bo2(b):
                pool.wait_ge(s_x1, b + 1)
                for c in range(b * C, (b + 1) * C):
                    nc.gpsimd.tensor_tensor(x1_bo[:, c, :], x1[:, c, :], bo2[:, :], ALU.add).then_inc(s_x1bo, 1)

            def divide1(s):
                for r in range(2):
                    pool.wait_ge(s_rec1, 2 * s + r + 1)
                    pr = prob1[:, s % 3, r, :].rearrange("p (c i) -> p c i", c=C)
                    nc.gpsimd.tensor_tensor(pr, pr, rec1[:, s % 2, r, :].unsqueeze(2).to_broadcast([P, C, S]),
                                            ALU.mult).then_inc(s_norm1, 1)

            for g in range(LAST_G + 2):
                n = g - N_SELF
                if 1 <= g <= N_SELF:
                    divide1(g - 1)
                for kind, b in BETWEEN.get(g, ()):
                    if kind == "residual":
                        reciprocal_std(1 + b, b * C, C)
                        add_bo2(b)
                    elif kind == "residual2":
                        reciprocal_std(3 + b, b * C, C)
                    elif kind == "turned2":
                        split_tokens(b)
                if 0 <= n - SPLIT_N < 2 * (NE + 1):
                    split_weights(n - SPLIT_N)
            reciprocal_std(4, C, C)
            for i in range(N_FFN):
                b, k = divmod(i, NE + 1)
                for kind, row in FFN_BETWEEN.get(i + LAG_D, ()):
                    if kind == "turned2":
                        split_tokens(row)
                if 1 <= k < NE:
                    pool.wait_ge(s_ypart, i + 1)
                    if k > 1:
                        pool.wait_ge(s_acc, b * (NE - 1) + k - 1)
                    sums = acc[:, b * C:(b + 1) * C, :]
                    nc.gpsimd.tensor_tensor(sums, sums, y_part[k % 2], ALU.add).then_inc(s_acc, 1)

        @block.scalar
        def _(act):
            act.dma_start(biases[:, :], a["biases"]).then_inc(d_bias, 16)
            act.wait_ge(d_bias, 16)
            nc.scalar.mul(bq1_s[:, :], bias1[:, 0, :], -SCALE1).then_inc(s_bq, 1)

            def evacuate(j, kind, which):
                act.wait_ge(s_item, j + 1)
                bank = ps[:, j % 8, :]
                if kind == "ctx_t":
                    ins = nc.scalar.copy(ctx_t[:, which * BANK:(which + 1) * BANK], bank)
                elif kind == "kx":
                    ins = nc.scalar.activation(k2_t[:, which * BANK:(which + 1) * BANK], bank, ACT.Identity,
                                               bias=bias2[:, 1:2])
                elif kind == "vx":
                    ins = nc.scalar.copy(v2[:, which * KC:(which + 1) * KC, :, 0:HD2],
                                         bank.rearrange("p (c h d) -> p c h d", c=KC, h=H2))
                elif kind == "q":
                    if which == 0:
                        act.wait_ge(s_bq, 1)
                    ins = nc.scalar.activation(q1_t[:, which, :], bank, ACT.Identity,
                                               bias=bq1_s[:, which:which + 1], scale=-SCALE1)
                ins.then_inc(s_ev["act"], 1)

            for j, (kind, which, engine) in enumerate(ITEMS):
                if engine == "act":
                    evacuate(j, kind, which)

            def x_hat_evac(k, b):
                act.wait_ge(s_xhat_ps, k)
                nc.scalar.copy(x_hat_t[:, b * S:(b + 1) * S], ps[:, MID_BANK, 0:S]).then_inc(s_xhat_t, 1)

            act.wait_ge(d_kdram, 16)
            def between(what):
                kind, b = what
                if kind == "turned":
                    x_hat_evac(1 + b, b)
                elif kind == "turned2":
                    x_hat_evac(3 + b, b)
                elif kind == "turned_o2":
                    act.wait_ge(s_o2turn, b + 1)
                    nc.scalar.copy(o2_t[:, :], ps[:, MID_BANK, S:2 * S]).then_inc(s_o2t, 1)
                elif kind == "gate_exp":
                    act.wait_ge(s_lshift, b + 1)
                    nc.scalar.activation(gate_e[:, b * C:(b + 1) * C, :], logit[:, b * C:(b + 1) * C, :], ACT.Exp
                                         ).then_inc(s_gexp, 1)

            def exp1(s):
                for r in range(2):
                    act.wait_ge(s_low1, 2 * s + r + 1)
                    if s >= 2:
                        act.wait_ge(s_rec1, 2 * (s - 2) + r + 1)
                    if s >= 3:
                        act.wait_ge(s_turn1, 2 * (s - 3) + r + 1)
                    for c in range(C):
                        e = nc.scalar.activation(prob1[:, s % 3, r, c * S:(c + 1) * S],
                                                 ps[:, 2 * (s % 2) + r, c * S:(c + 1) * S], ACT.Exp,
                                                 bias=low1[:, s % 2, r, c:c + 1], scale=-1.0,
                                                 accum_out=sum1[:, s % 2, r, c:c + 1])
                    e.then_inc(s_exp1, 1)

            def silu_step(i):
                act.wait_ge(s_g, i + 1)
                if i >= 2:
                    act.wait_ge(s_hid, i - 1)
                nc.scalar.activation(silu[i % 2], ps[:, i % 2, :], ACT.Silu).then_inc(s_silu, 1)
                for what in FFN_BETWEEN.get(i, ()):
                    between(what)

            def values_evac(g):
                for i, (c, half) in enumerate(V_ITEMS[g]):
                    if half == 0:
                        act.wait_ge(s_v, len(V_BANKS) * g + i + 1)
                        nc.scalar.copy(v1[:, c, 0:BANK], ps[:, V_BANKS[i], :]).then_inc(s_vev[0], 1)

            def exp2(n):
                for c in range(C):
                    act.wait_ge(s_low2, C * n + c + 1)
                    if n >= 3 and c == 0:
                        act.wait_ge(s_turn2b, n - 2)
                    nc.scalar.activation(prob2[n % 3][:, c, :], score2[n % 2][:, c, :], ACT.Exp,
                                         bias=low2[:, n % 2, c:c + 1], scale=-1.0).then_inc(s_exp2, 1)

            for g in range(LAST_G + 2):
                n = g - N_SELF
                if g == 0:
                    values_evac(g)
                for what in BETWEEN.get(g, ()):
                    between(what)
                if g < N_SELF:
                    exp1(g)
                if g == 1:
                    values_evac(g)
                if n in O_READY:
                    k = O_READY[n]
                    act.wait_ge(s_pv2, k + 1)
                    if k >= 1:
                        act.wait_ge(s_oturn, k)
                    nc.scalar.copy(o_raw[:, :], ps[:, O2_BANK[k], 0:S]).then_inc(s_oraw, 1)
                if 0 <= n < N_CROSS:
                    exp2(n)
                if 0 <= g - LAG_V < N_SELF:
                    b, p = divmod(g - LAG_V, NP)
                    act.wait_ge(s_pv1, g - LAG_V + 1)
                    nc.scalar.activation(o1_t[:, b, p, :], ps[:, O_BANK, 0:S], ACT.Identity,
                                         bias=bias1[:, 2, p:p + 1]).then_inc(s_o1, 1)
                if 0 <= n - LAG_T < N_CROSS:
                    act.wait_ge(s_turn2b, n - LAG_T + 1)
                    nc.scalar.copy(prob2_t[(n - LAG_T) % PT_SLOTS][:, 2:4, :],
                                   ps[:, PT_BANK + 1, :].rearrange("p (k t) -> p k t", k=2)).then_inc(s_pt2b, 1)
                if FFN_G <= g < FFN_G + FFN_EARLY:
                    silu_step(g - FFN_G)

            for i in range(FFN_EARLY, N_FFN):
                silu_step(i)

        @block.tensor
        def _(pe):
            mm, turn = nc.tensor.matmul, nc.tensor.transpose
            pe.wait_ge(s_ident, 1)
            for _ in range(WARM_UP):
                mm(ps[:, MID_BANK, 0:P], ident[:, :], ident[:, :], start=True, stop=True)
            for j, (kind, which, _) in enumerate(ITEMS):
                bank = ps[:, j % 8, :]
                if j >= 8:
                    engine, value = evacuated(j - 8)
                    pe.wait_ge(s_ev[engine], value)
                if kind == "ctx_t":
                    pe.wait_ge(d_ctx[which], 16)
                    for c in range(KC):
                        last = turn(bank[:, c * P:(c + 1) * P], ctx_in[:, which * KC + c, :], ident[:, :])
                elif kind == "kx":
                    if which == 0:
                        pe.wait_ge(d_wk2, 16)
                        pe.wait_ge(s_ev["act"], 2)
                    last = mm(bank, wk2[:, :], ctx_t[:, which * BANK:(which + 1) * BANK], start=True, stop=True)
                elif kind == "vx":
                    if which == 0:
                        pe.wait_ge(d_wv2, 16)
                    for c in range(KC):
                        t = (which * KC + c) * P
                        last = mm(bank[:, c * P:(c + 1) * P], ctx_t[:, t:t + P], wv2[:, :], start=True, stop=True)
                elif kind == "x_t":
                    pe.wait_ge(s_xhat, 1)
                    for c in range(NC_):
                        last = turn(bank[:, c * P:(c + 1) * P], x_hat[:, c, :], ident[:, :])
                else:
                    if which == 0:
                        pe.wait_ge(d_wq1 if kind == "q" else d_wk1, 16)
                    if kind == "q" and which == 0:
                        pe.wait_ge(s_ev["dve"], evacuated(index_of("x_t", 0))[1])
                    w = wq1 if kind == "q" else wk1
                    last = mm(bank, w[:, which * P:(which + 1) * P], x_hat_t[:, :], start=True, stop=True)
                last.then_inc(s_item, 1)

            def out_proj1(b, p):
                if p == 0:
                    if b == 0:
                        pe.wait_ge(d_wo1, 16)
                    else:
                        pe.wait_ge(s_qparts, 1)
                pe.wait_ge(s_o1, NP * b + p + 1)
                for c in range(C):
                    last = mm(ps[:, MID_BANK, c * P:(c + 1) * P], o1_t[:, b, p, c * P:(c + 1) * P], wo1[:, p, :],
                              start=p == 0 and c == 0, stop=p == NP - 1 and c == C - 1)
                if p == NP - 1:
                    last.then_inc(s_wo, 1)

            def out_proj2(b):
                if b == 0:
                    pe.wait_ge(d_wo2, 16)
                pe.wait_ge(s_o2t, b + 1)
                for c in range(C):
                    last = mm(ps[:, MID_BANK, c * P:(c + 1) * P], o2_t[:, c * P:(c + 1) * P], wo2[:, :],
                              start=True, stop=True)
                last.then_inc(s_wo, 1)

            def turn_o2(b):
                if b == 1:
                    pe.wait_ge(s_lshift, 1)
                pe.wait_ge(s_o2, NG * (b + 1))
                for c in range(C):
                    last = turn(ps[:, MID_BANK, S + c * P:S + (c + 1) * P], o2[:, b * C + c, :], ident[:, :])
                last.then_inc(s_o2turn, 1)

            def turn_x_hat(k, b):
                pe.wait_ge(s_xhat, k + 1)
                for c in range(C):
                    last = turn(ps[:, MID_BANK, c * P:(c + 1) * P], x_hat[:, b * C + c, :], ident[:, :])
                last.then_inc(s_xhat_ps, 1)

            def query2(b):
                if b == 0:
                    pe.wait_ge(d_wq2, 16)
                pe.wait_ge(s_xhat_t, b + 1)
                mm(ps[:, MID_BANK, S:2 * S], wq2[:, :], x_hat_t[:, b * S:(b + 1) * S],
                   start=True, stop=True).then_inc(s_q2ps, 1)

            def gate(b):
                if b == 0:
                    pe.wait_ge(d_ffn, 16 * 5)
                pe.wait_ge(s_xhat_t, 3 + b)
                for c in range(C):
                    t = b * S + c * P
                    last = mm(ps[:, MID_BANK, S + c * NE:S + (c + 1) * NE], x_hat_t[:, t:t + P], gate_w[:, :],
                              start=True, stop=True)
                last.then_inc(s_logit, 1)

            def between(what):
                kind, b = what
                if kind == "turn":
                    turn_x_hat(1 + b, b)
                elif kind == "q":
                    query2(b)
                elif kind == "turn_o2":
                    turn_o2(b)
                elif kind == "wo2":
                    out_proj2(b)
                elif kind == "turn2":
                    turn_x_hat(3 + b, b)
                elif kind == "gate":
                    gate(b)

            def scores1(s):
                b, p = divmod(s, NP)
                for r in range(2):
                    if s >= 2:
                        pe.wait_ge(s_exp1, 2 * (s - 2) + r + 1)
                    rows = slice(HD1 * r, HD1 * (r + 1))
                    for c in range(C):
                        last = mm(ps[:, 2 * (s % 2) + r, c * S:(c + 1) * S],
                                  q1_t[rows, p, b * S + c * P:b * S + (c + 1) * P],
                                  k1_t[rows, p, b * S:(b + 1) * S], start=True, stop=True)
                    last.then_inc(s_score1, 1)

            def values1(s):
                b, p = divmod(s, NP)
                pe.wait_ge(s_pt1, 2 * (s + 1))
                if s >= 1:
                    pe.wait_ge(s_o1, s)
                for c in range(C):
                    for r in range(2):
                        h = 2 * p + r
                        last = mm(ps[HD1 * r:HD1 * (r + 1), O_BANK, 0:S],
                                  v1[:, b * C + c, h * HD1:(h + 1) * HD1],
                                  prob1_t[:, s % 2, r, c * S:(c + 1) * S], start=c == 0, stop=c == C - 1)
                last.then_inc(s_pv1, 1)

            def turn1(s):
                for r in range(2):
                    pe.wait_ge(s_norm1, 2 * s + r + 1)
                    if s >= 1:
                        pe.wait_ge(s_pt1, 2 * (s - 1) + r + 1)
                    elif r == 0:
                        pe.wait_ge(s_vev[0], NC_)
                        pe.wait_ge(s_vev[1], NC_)
                    for c in range(C):
                        for i in range(C):
                            last = turn(ps[:, PT_BANK + r, i * S + c * P:i * S + (c + 1) * P],
                                        prob1[:, s % 3, r, c * S + i * P:c * S + (i + 1) * P], ident[:, :])
                    last.then_inc(s_turn1, 1)

            def scores2(n):
                b, h = divmod(n, H2)
                if n == 0:
                    pe.wait_ge(d_kstack, 16 * PARTS * PARTS)
                if h == 0:
                    pe.wait_ge(d_qstack[b], 16 * PARTS)
                for c in range(C):
                    if n >= 2:
                        pe.wait_ge(s_low2, C * (n - 2) + c + 1)
                    else:
                        pe.wait_ge(s_exp1, 2 * (N_SELF - 2 + n) + c + 1)
                    t = b * S + c * P
                    mm(ps[:, 2 * (n % 2) + c, :], q2_stack[:, h, t:t + P],
                       k2_stack[:, h, b * SK:(b + 1) * SK], start=True, stop=True).then_inc(s_score2, 1)

            def values2(k, kc):
                b, hg = divmod(k, NG)
                if kc == 0:
                    pe.wait_ge(s_pt2a, HG * (k + 1))
                    pe.wait_ge(s_pt2b, HG * (k + 1))
                    if k == B * NG - 1:
                        pe.wait_ge(s_lshift, 1)
                    elif k >= 1:
                        pe.wait_ge(s_o2, k)
                    else:
                        pe.wait_ge(s_o1, N_SELF)
                        pe.wait_ge(s_const, 1 + NE)
                        pe.wait_ge(s_v2, B * KC)
                for g in range(HG):
                    last = mm(ps[CW * g:CW * (g + 1), O2_BANK[k], 0:S], v2[:, b * KC + kc, HG * hg + g, :],
                       prob2_t[(HG * k + g) % PT_SLOTS][:, kc, :], start=kc == 0, stop=kc == KC - 1)
                if kc == KC - 1:
                    last.then_inc(s_pv2, 1)

            def turn_outputs2(k):
                pe.wait_ge(s_oraw, k + 1)
                for c in range(C):
                    last = turn(ps[:, O2_BANK[k], S + c * P:S + (c + 1) * P], o_raw[:, c * P:(c + 1) * P], ident[:, :])
                last.then_inc(s_oturn, 1)

            def turn2(n):
                pe.wait_ge(s_exp2, C * (n + 1))
                for half, done, free in ((0, s_turn2a, s_pt2a), (1, s_turn2b, s_pt2b)):
                    if n >= 1:
                        pe.wait_ge(free, n)
                    else:
                        pe.wait_ge(s_pt1, 2 * N_SELF)
                    for k2 in range(2):
                        kc = 2 * half + k2
                        for c in range(C):
                            last = turn(ps[:, PT_BANK + half, k2 * S + c * P:k2 * S + (c + 1) * P],
                                        prob2[n % 3][:, c, kc * P:(kc + 1) * P], ident[:, :])
                    last.then_inc(done, 1)

            def values_of_tokens(g):
                for i, (c, half) in enumerate(V_ITEMS[g]):
                    if g == 0:
                        if i == 0:
                            pe.wait_ge(s_vparts, 2)
                        engine, value = evacuated(max(j for j in range(len(ITEMS)) if j % 8 == V_BANKS[i]))
                        pe.wait_ge(s_ev[engine], value)
                    else:
                        pe.wait_ge(s_vev[half], 2 * (g - 1) + i // 2 + 1)
                    for j, (xi, wi) in enumerate(BIG_PARTS):
                        last = mm(ps[:, V_BANKS[i], :], xv_parts[:, xi, c * P:(c + 1) * P],
                                  wv1_parts[:, wi, half * BANK:(half + 1) * BANK],
                                  start=j == 0, stop=j == len(BIG_PARTS) - 1)
                    last.then_inc(s_v, 1)

            def expert_step(i):
                if i == 0:
                    pe.wait_ge(s_low2, C * N_CROSS)
                if i < N_FFN:
                    b, k = divmod(i, NE + 1)
                    e, rows = (k - 1) % (NE + 1), slice(b * S, (b + 1) * S)
                    if i >= 2:
                        pe.wait_ge(s_silu, i - 1)
                    if k == 0:
                        pe.wait_ge(s_xparts, b + 1)
                    if i == 0:
                        pe.wait_ge(s_wparts, 2 * (NE + 1))

                    def up(bank, which):
                        for f in range(FC):
                            for j, (wi, xi) in enumerate(BIG_PARTS):
                                last = mm(ps[:, bank, f * S:(f + 1) * S],
                                          w_parts[which][e][wi][:, f * P:(f + 1) * P], x_parts[b][xi][:, :],
                                          start=j == 0, stop=j == len(BIG_PARTS) - 1)
                        return last

                    up(i % 2, 0).then_inc(s_g, 1)
                    if i >= 2:
                        pe.wait_ge(s_hid, i - 1)
                    up(2 + i % 2, 1).then_inc(s_u, 1)
                if i >= LAG_D:
                    j = i - LAG_D
                    e = (j % (NE + 1) - 1) % (NE + 1)
                    if j == 0:
                        pe.wait_ge(s_pt2a, N_CROSS)
                        pe.wait_ge(s_pt2b, N_CROSS)
                        pe.wait_ge(d_wd, 32)
                    pe.wait_ge(s_hid, j + 1)
                    if j >= 2:
                        pe.wait_ge(s_ypart, j - 1)
                    for c in range(C):
                        for f in range(FC):
                            last = mm(ps[:, 4 + j % 2, c * P:(c + 1) * P],
                                      hid[j % 3][:, f, c * P:(c + 1) * P], wd[:, e, f, :],
                                      start=f == 0, stop=f == FC - 1)
                    last.then_inc(s_y, 1)
                for what in FFN_BETWEEN.get(i, ()):
                    between(what)

            for g in range(LAST_G + 1):
                n = g - N_SELF
                if g == 0:
                    values_of_tokens(0)
                if g < N_SELF:
                    scores1(g)
                if 1 <= n + 1 < N_CROSS:
                    scores2(n + 1)
                if g >= 1 and g in V_ITEMS:
                    values_of_tokens(g)
                for b, p in WO1.get(g, ()):
                    out_proj1(b, p)
                for what in BETWEEN.get(g, ()):
                    between(what)
                if 0 <= g - LAG_T < N_SELF:
                    turn1(g - LAG_T)
                if 0 <= n - LAG_T < N_CROSS:
                    turn2(n - LAG_T)
                if 0 <= g - LAG_V < N_SELF:
                    values1(g - LAG_V)
                if n + 1 == 0:
                    scores2(0)
                if FFN_G <= g < FFN_G + FFN_EARLY:
                    expert_step(g - FFN_G)
                if n in O_READY:
                    turn_outputs2(O_READY[n])
                for k, kc in VALUES2.get(n, ()):
                    values2(k, kc)

            for i in range(FFN_EARLY, N_FFN + LAG_D):
                expert_step(i)

        @block.vector
        def _(dve):
            chain = [0]

            def link(ins):
                chain[0] += 1
                ins.then_inc(s_dve, 1)
                dve.wait_ge(s_dve, chain[0])

            def statistics(k, src, first, count):
                for c in range(first, first + count):
                    ins = nc.vector.bn_stats(stats[:, c, :], src[:, c, :])
                link(ins)
                for c in range(first, first + count):
                    ins = nc.vector.bn_aggr(mean_var[:, c, :], stats[:, c, :])
                ins.then_inc(s_var, 1)

            def normalise(k, src, first, count):
                dve.wait_ge(s_var, k + 1)
                dve.wait_ge(s_rstd, k + 1)
                for c in range(first, first + count):
                    ins = nc.vector.tensor_scalar(x_hat[:, c, :], src[:, c, :], mean_var[:, c, 0:1],
                                                  rstd[:, c:c + 1], ALU.subtract, ALU.mult)
                ins.then_inc(s_xhat, 1)

            dve.wait_ge(d_x, 16)
            statistics(0, x_in, 0, NC_)
            normalise(0, x_in, 0, NC_)

            def split(full, rest_, parts):
                link(nc.vector.tensor_copy(parts[:, 0, :], full))
                link(nc.vector.tensor_tensor(rest_, full, parts[:, 0, :], ALU.subtract))
                link(nc.vector.tensor_copy(parts[:, 1, :], rest_))
                return nc.vector.tensor_tensor(parts[:, 2, :], rest_, parts[:, 1, :], ALU.subtract)

            for j, (kind, which, engine) in enumerate(ITEMS):
                if engine != "dve":
                    continue
                if (kind, which) == ("k", 0):
                    dve.wait_ge(d_bias, 16)
                dve.wait_ge(s_item, j + 1)
                bank = ps[:, j % 8, :]
                if kind == "x_t":
                    ins = nc.vector.tensor_copy(x_hat_t[:, :], bank)
                else:
                    ins = nc.vector.tensor_scalar(k1_t[:, which, :], bank, bias1[:, 1, which:which + 1], None, ALU.add)
                ins.then_inc(s_ev["dve"], 1)
                if (kind, which) == ("k", 1):
                    dve.wait_ge(s_ev["act"], evacuated(index_of("kx", 1))[1])
                    split(k2_t, k2_rest, k2_parts).then_inc(s_kparts, 1)
                if (kind, which) == ("k", 4):
                    dve.wait_ge(d_mask, 16)
                    nc.vector.tensor_scalar(mask_add[:, :, :], mask_in, 0, MASKED, ALU.is_equal, ALU.mult
                                            ).then_inc(s_maskadd, 1)

            def residual(k, b, dst, src, done):
                dve.wait_ge(s_wo, k + 1)
                ins = nc.vector.tensor_tensor(dst[:, b * C:(b + 1) * C, :],
                                              ps[:, MID_BANK, 0:C * P].rearrange("p (c n) -> p c n", c=C),
                                              src[:, b * C:(b + 1) * C, :], ALU.add)
                ins.then_inc(done, 1)
                dve.wait_ge(done, b + 1)

            def between(what):
                kind, b = what
                if kind == "residual":
                    dve.wait_ge(s_xbo, C * (b + 1))
                    residual(b, b, x1, x_bo, s_x1)
                    statistics(1 + b, x1, b * C, C)
                elif kind == "x_hat":
                    normalise(1 + b, x1, b * C, C)
                elif kind == "parts":
                    dve.wait_ge(s_q2ps, b + 1)
                    if b >= 1:
                        dve.wait_ge(d_qdram[b - 1], 16)
                    link(nc.vector.tensor_scalar(q2_t[:, :], ps[:, MID_BANK, S:2 * S], bias2[:, 0:1], -SCALE2,
                                                 ALU.add, ALU.mult))
                    split(q2_t[:, :], q2_rest[:, :], q2_parts).then_inc(s_qparts, 1)
                elif kind == "residual2":
                    dve.wait_ge(s_x1bo, C * (b + 1))
                    residual(2 + b, b, x2, x1_bo, s_x2)
                    statistics(3 + b, x2, b * C, C)
                elif kind == "x_hat2":
                    normalise(3 + b, x2, b * C, C)
                elif kind == "shift":
                    shift_logits(b)
                elif kind == "weights":
                    gate_weights(b)

            v = nc.vector

            def rows_of(b):
                return slice(b * C, (b + 1) * C)

            def wide(i, b):
                return col[:, i, rows_of(b)].unsqueeze(2).to_broadcast([P, C, NE])

            def shift_logits(b):
                cs = rows_of(b)
                dve.wait_ge(s_logit, b + 1)
                link(v.tensor_copy(logit[:, cs, :],
                                   ps[:, MID_BANK, S:S + C * NE].rearrange("p (c e) -> p c e", c=C)))
                link(v.tensor_reduce(col[:, 0, cs], logit[:, cs, :], AX.X, ALU.max))
                v.tensor_tensor(logit[:, cs, :], logit[:, cs, :], wide(0, b), ALU.subtract).then_inc(s_lshift, 1)

            def gate_weights(b):
                cs = rows_of(b)
                dve.wait_ge(s_gexp, b + 1)
                link(v.tensor_reduce(col[:, 1, cs], gate_e[:, cs, :], AX.X, ALU.add))
                link(v.reciprocal(col[:, 2, cs], col[:, 1, cs]))
                link(v.tensor_tensor(gate_s[:, cs, :], gate_e[:, cs, :], wide(2, b), ALU.mult))

                def first_largest(values, to):
                    link(v.tensor_reduce(col[:, 3, cs], values, AX.X, ALU.max))
                    link(v.tensor_tensor(pick[:, cs, :], values, wide(3, b), ALU.is_equal))
                    link(v.tensor_tensor(pick[:, cs, :], pick[:, cs, :], rank[:, cs, :], ALU.mult))
                    link(v.tensor_reduce(col[:, 4, cs], pick[:, cs, :], AX.X, ALU.max))
                    link(v.tensor_tensor(to, pick[:, cs, :], wide(4, b), ALU.is_equal))

                first_largest(gate_s[:, cs, :], pick1[:, cs, :])
                link(v.scalar_tensor_tensor(out=rest[:, cs, :], in0=pick1[:, cs, :], scalar=-2.0,
                                            in1=gate_s[:, cs, :], op0=ALU.mult, op1=ALU.add))
                first_largest(rest[:, cs, :], pick2[:, cs, :])
                link(v.tensor_tensor(pick[:, cs, :], pick1[:, cs, :], pick2[:, cs, :], ALU.add))
                link(v.tensor_tensor(pick[:, cs, :], pick[:, cs, :], gate_s[:, cs, :], ALU.mult))
                link(v.tensor_reduce(col[:, 5, cs], pick[:, cs, :], AX.X, ALU.add))
                link(v.tensor_scalar(col[:, 5, cs], col[:, 5, cs], 1e-20, None, ALU.add))
                link(v.reciprocal(col[:, 0, cs], col[:, 5, cs]))
                link(v.tensor_tensor(w_e[:, cs, :], pick[:, cs, :], wide(0, b), ALU.mult))

            def low_scores1(s):
                for r in range(2):
                    dve.wait_ge(s_score1, 2 * s + r + 1)
                    nc.vector.tensor_reduce(low1[:, s % 2, r, :],
                                            ps[:, 2 * (s % 2) + r, :].rearrange("p (c i) -> p c i", c=C),
                                            AX.X, ALU.min).then_inc(s_low1, 1)

            def low_scores2(n):
                for c in range(C):
                    dve.wait_ge(s_score2, C * n + c + 1)
                    if n >= 2:
                        dve.wait_ge(s_exp2, C * (n - 2) + c + 1)
                    nc.vector.tensor_tensor_reduce(out=score2[n % 2][:, c, :], in0=ps[:, 2 * (n % 2) + c, :],
                                                   in1=mask_add[:, c, :], scale=1.0, scalar=3e38,
                                                   op0=ALU.add, op1=ALU.min, accum_out=low2[:, n % 2, c:c + 1]
                                                   ).then_inc(s_low2, 1)

            def values_evac(g):
                for i, (c, half) in enumerate(V_ITEMS[g]):
                    if half == 1:
                        dve.wait_ge(s_v, len(V_BANKS) * g + i + 1)
                        nc.vector.tensor_copy(v1[:, c, BANK:2 * BANK], ps[:, V_BANKS[i], :]).then_inc(s_vev[1], 1)

            def bank_y(i):
                return ps[:, 4 + i % 2, 0:C * D].rearrange("p (c n) -> p c n", c=C)

            def outputs(i):
                b, k = divmod(i, NE + 1)
                cs = rows_of(b)
                dve.wait_ge(s_y, i + 1)
                if k == 0:
                    v.tensor_tensor(acc[:, cs, :], bank_y(i), x2[:, cs, :], ALU.add).then_inc(s_ypart, 1)
                elif k < NE:
                    if k >= 3:
                        dve.wait_ge(s_acc, b * (NE - 1) + k - 2)
                    v.tensor_tensor(y_part[k % 2], bank_y(i), w_e[:, cs, k - 1:k].to_broadcast([P, C, D]),
                                    ALU.mult).then_inc(s_ypart, 1)
                else:
                    dve.wait_ge(s_acc, (b + 1) * (NE - 1))
                    for c in range(C):
                        ins = v.scalar_tensor_tensor(out=y_out[:, b * C + c, :], in0=bank_y(i)[:, c, :],
                                                     scalar=w_e[:, b * C + c, k - 1:k], in1=acc[:, b * C + c, :],
                                                     op0=ALU.mult, op1=ALU.add)
                    ins.then_inc(s_ypart, 1)

            def hidden_step(i):
                if i < N_FFN:
                    dve.wait_ge(s_silu, i + 1)
                    dve.wait_ge(s_u, i + 1)
                    if i >= 3:
                        dve.wait_ge(s_y, i - 2)
                    v.tensor_tensor(hid[i % 3], silu[i % 2].rearrange("p (f t) -> p f t", f=FC),
                                    ps[:, 2 + i % 2, :].rearrange("p (f t) -> p f t", f=FC), ALU.mult
                                    ).then_inc(s_hid, 1)
                if i >= LAG_D:
                    outputs(i - LAG_D)
                for what in FFN_BETWEEN.get(i, ()):
                    between(what)

            dve.wait_ge(s_maskadd, 1)
            dve.wait_ge(s_const, 1 + NE)
            for g in range(LAST_G + 1):
                n = g - N_SELF
                if 1 <= g <= N_SELF:
                    for r in range(2):
                        dve.wait_ge(s_exp1, 2 * (g - 1) + r + 1)
                        nc.vector.reciprocal(rec1[:, (g - 1) % 2, r, :], sum1[:, (g - 1) % 2, r, :]
                                             ).then_inc(s_rec1, 1)
                if g == 0:
                    values_evac(g)
                if g < N_SELF:
                    low_scores1(g)
                if g == 1:
                    values_evac(g)
                if 0 <= n < N_CROSS:
                    low_scores2(n)
                for what in BETWEEN.get(g, ()):
                    between(what)
                if 0 <= g - LAG_T < N_SELF:
                    for r in range(2):
                        dve.wait_ge(s_turn1, 2 * (g - LAG_T) + r + 1)
                        nc.vector.tensor_copy(prob1_t[:, g % 2, r, :], ps[:, PT_BANK + r, :]).then_inc(s_pt1, 1)
                if 0 <= n - LAG_T < N_CROSS:
                    dve.wait_ge(s_turn2a, n - LAG_T + 1)
                    nc.vector.tensor_copy(prob2_t[(n - LAG_T) % PT_SLOTS][:, 0:2, :],
                                          ps[:, PT_BANK, :].rearrange("p (k t) -> p k t", k=2)).then_inc(s_pt2a, 1)
                if n in O_READY:
                    k = O_READY[n]
                    b, hg = divmod(k, NG)
                    dve.wait_ge(s_oturn, k + 1)
                    o = ps[:, O2_BANK[k], S:2 * S].rearrange("p (c g d) -> p c g d", c=C, g=HG)
                    link(nc.vector.reciprocal(rec2[:, :, :], o[:, :, :, HD2]))
                    nc.vector.tensor_tensor(
                        o2[:, b * C:(b + 1) * C, hg * HG * HD2:(hg + 1) * HG * HD2].rearrange("p c (g d) -> p c g d", g=HG),
                        o[:, :, :, 0:HD2], rec2[:, :, :].unsqueeze(3).to_broadcast([P, C, HG, HD2]), ALU.mult
                        ).then_inc(s_o2, 1)
                if FFN_G <= g < FFN_G + FFN_EARLY:
                    hidden_step(g - FFN_G)

            for i in range(FFN_EARLY, N_FFN + LAG_D):
                hidden_step(i)


INPUTS = ["x", "ctx_1024", "mask_1x1xSxS2_ik1", "biases"]
INPUTS += ["L0_attn_" + w for w in ("Wq", "Wk", "Wv", "Wo", "bo")]
INPUTS += ["L0_xattn_" + w for w in ("Wq", "Wk", "Wv", "Wo", "bv", "bo")]
INPUTS += ["L0_ffn_" + w for w in ("gate_w", "w_gate", "w_up", "w_down", "ws_gate", "ws_up", "ws_down")]


def kernel(**inputs):
    import numpy as np
    import concourse.bacc as bacc
    from concourse.bass_utils import run_bass_kernel_spmd

    nc = bacc.Bacc("TRN2", target_bir_lowering=False, num_devices=1)
    laid = dict(inputs)
    columns = [np.asarray(inputs["L0_attn_" + w]).reshape(NP, P).T for w in ("bq", "bk", "bv")]
    columns += [np.asarray(inputs["L0_xattn_" + w]).reshape(H2, HD2).T.reshape(P, 1) for w in ("bq", "bk")]
    for w in ("L0_xattn_Wq", "L0_xattn_Wk"):
        laid[w] = np.asarray(inputs[w]).reshape(D, H2, HD2).transpose(0, 2, 1).reshape(D, D)
    laid["biases"] = np.concatenate(columns, axis=1)
    arrays, aps = {}, {}
    for name in INPUTS:
        array = np.ascontiguousarray(laid[name])
        arrays[f"in_{name}"] = array
        aps[name] = nc.dram_tensor(f"in_{name}", array.shape, mybir.dt.from_np(array.dtype), kind="ExternalInput").ap()
    out = nc.dram_tensor("out", (B, S, D), F32, kind="ExternalOutput").ap()
    build(nc, aps, out)
    return run_bass_kernel_spmd(nc, [arrays], core_ids=[0]).results[0]["out"]
```
